# Optimizing a Trainium2 kernel written in Bass

```python
import numpy as np
import jax
import jax.numpy as jnp

def _softmax(x, axis=-1):
    return jax.nn.softmax(x, axis=axis)

def _gelu(x):
    return jax.nn.gelu(x, approximate=True)

def _silu(x):
    return jax.nn.silu(x)

def _sigmoid(x):
    return jax.nn.sigmoid(x)

def _layernorm(x, axis=-1, eps=1e-05):
    m = jnp.mean(x, axis=axis, keepdims=True)
    v = jnp.var(x, axis=axis, keepdims=True)
    return (x - m) / jnp.sqrt(v + eps)

def _scatter_add(tgt, idx, src, axis=0):
    return tgt.at[idx].add(src)

def _segment_sum(src, seg, n):
    return jax.ops.segment_sum(src, seg, n)
kernel_name = 'mk_adj_resnorm_d2_adj_r2_2bbd15'

def setup_inputs(seed: int=0):
    np.random.seed(seed)
    _w = jnp.asarray

    def _rec_inputs():
        import jax
        import jax.numpy as jnp
        _gk = jax.random.key(seed)
        x = -0.0002928 + 1 * jax.random.normal(jax.random.fold_in(_gk, 1), (16, 512, 256), jnp.float32)
        _w = (1.0 + jnp.arange(512, dtype=jnp.float32)) ** (-0.5)
        _w = _w / _w.mean()
        _pij = jnp.clip(0.00390625 * _w[:, None] * _w[None, :], 0.0, 1.0)
        _a = jax.random.uniform(jax.random.fold_in(_gk, 2), (16, 512, 512)) < _pij
        adj = _a.astype(jnp.int32)
        return (x, adj)
    x, adj = _rec_inputs()

    def _L0_gnn_setup():
        import jax, jax.numpy as jnp
        import numpy as np
        L = 3
        D = 256
        B, N = (8, 512)
        EPS = 1e-05

        def layernorm(x, gamma, beta):
            mu = jnp.mean(x, axis=-1, keepdims=True)
            var = jnp.var(x, axis=-1, keepdims=True)
            return (x - mu) * jax.lax.rsqrt(var + EPS) * gamma + beta
        key = jax.random.key(seed)
        ks = jax.random.split(key, 12)
        s = 1.0 / np.sqrt(D)
        node_features = jax.random.normal(ks[0], (B, N, D), dtype=jnp.float32)
        adjacency_matrix = jax.random.randint(ks[1], (B, N, N), 0, 2, dtype=jnp.int32)
        return {'node_features': node_features, 'adjacency_matrix': adjacency_matrix, 'attn_w': jax.random.normal(ks[2], (L, 2 * D), dtype=jnp.float32) * (1.0 / np.sqrt(2 * D)), 'attn_b': jax.random.normal(ks[3], (L,), dtype=jnp.float32) * 0.01, 'W1': jax.random.normal(ks[4], (L, D, 4 * D), dtype=jnp.float32) * s, 'b1': jnp.zeros((L, 4 * D), dtype=jnp.float32), 'W2': jax.random.normal(ks[5], (L, 4 * D, D), dtype=jnp.float32) * (1.0 / np.sqrt(4 * D)), 'b2': jnp.zeros((L, D), dtype=jnp.float32), 'g1': jnp.ones((L, D), dtype=jnp.float32), 'beta1': jnp.zeros((L, D), dtype=jnp.float32), 'g2': jnp.ones((L, D), dtype=jnp.float32), 'beta2': jnp.zeros((L, D), dtype=jnp.float32)}
    _L0_gnn_all = _L0_gnn_setup()
    _L0_gnn_in = {k: v for k, v in _L0_gnn_all.items() if k in ('attn_w', 'attn_b', 'W1', 'b1', 'W2', 'b2', 'g1', 'beta1', 'g2', 'beta2')}
    del _L0_gnn_all

    def _L1_gnn_setup():
        import jax, jax.numpy as jnp
        import numpy as np
        NEG_INF = -1e+30
        NEG_SLOPE = 0.2
        key = jax.random.key(seed)
        k1, k2, k3, k4, k5 = jax.random.split(key, 5)
        B, N, D, H = (2, 1024, 256, 8)
        k = D // H
        return {'x': jax.random.normal(k1, (B, N, D), dtype=jnp.float32), 'A': jax.random.randint(k2, (B, N, N), 0, 2, dtype=jnp.int32), 'W_proj': jax.random.normal(k3, (D, D), dtype=jnp.float32) * (1.0 / np.sqrt(D)), 'W_att': jax.random.normal(k4, (H, 2 * k), dtype=jnp.float32) * (1.0 / np.sqrt(2 * k)), 'b_att': jax.random.normal(k5, (H,), dtype=jnp.float32) * 0.01}
    _L1_gnn_all = _L1_gnn_setup()
    _L1_gnn_in = {k: v for k, v in _L1_gnn_all.items() if k in ('W_proj', 'W_att', 'b_att')}
    del _L1_gnn_all
    return {'x': x, 'adj': adj, 'L0_gnn_attn_w': _L0_gnn_in['attn_w'], 'L0_gnn_attn_b': _L0_gnn_in['attn_b'], 'L0_gnn_W1': _L0_gnn_in['W1'], 'L0_gnn_b1': _L0_gnn_in['b1'], 'L0_gnn_W2': _L0_gnn_in['W2'], 'L0_gnn_b2': _L0_gnn_in['b2'], 'L0_gnn_g1': _L0_gnn_in['g1'], 'L0_gnn_beta1': _L0_gnn_in['beta1'], 'L0_gnn_g2': _L0_gnn_in['g2'], 'L0_gnn_beta2': _L0_gnn_in['beta2'], 'L1_gnn_W_proj': _L1_gnn_in['W_proj'], 'L1_gnn_W_att': _L1_gnn_in['W_att'], 'L1_gnn_b_att': _L1_gnn_in['b_att']}

def reference(x, adj, L0_gnn_attn_w, L0_gnn_attn_b, L0_gnn_W1, L0_gnn_b1, L0_gnn_W2, L0_gnn_b2, L0_gnn_g1, L0_gnn_beta1, L0_gnn_g2, L0_gnn_beta2, L1_gnn_W_proj, L1_gnn_W_att, L1_gnn_b_att):
    import jax
    import jax.numpy as jnp

    def _L0_gnn_ref(node_features, adjacency_matrix, attn_w, attn_b, W1, b1, W2, b2, g1, beta1, g2, beta2):
        import jax, jax.numpy as jnp
        import numpy as np
        L = 3
        D = 256
        B, N = (8, 512)
        EPS = 1e-05

        def layernorm(x, gamma, beta):
            mu = jnp.mean(x, axis=-1, keepdims=True)
            var = jnp.var(x, axis=-1, keepdims=True)
            return (x - mu) * jax.lax.rsqrt(var + EPS) * gamma + beta
        n = adjacency_matrix.shape[-1]
        mask = adjacency_matrix.astype(jnp.float32) + jnp.eye(n, dtype=jnp.float32) > 0
        x = node_features
        d = x.shape[-1]
        for l in range(attn_w.shape[0]):
            si = x @ attn_w[l, :d]
            sj = x @ attn_w[l, d:]
            scores = si[:, :, None] + sj[:, None, :] + attn_b[l]
            scores = jnp.where(scores >= 0, scores, 0.2 * scores)
            scores = jnp.where(mask, scores, -jnp.inf)
            attn = jax.nn.softmax(scores, axis=-1)
            agg = jnp.einsum('bij,bjd->bid', attn, x)
            h = layernorm(x + agg, g1[l], beta1[l])
            ff = jax.nn.gelu(h @ W1[l] + b1[l], approximate=False) @ W2[l] + b2[l]
            x = layernorm(h + ff, g2[l], beta2[l])
        return x

    def _L1_gnn_ref(x, A, W_proj, W_att, b_att):
        import jax, jax.numpy as jnp
        import numpy as np
        NEG_INF = -1e+30
        NEG_SLOPE = 0.2
        B, N, _ = x.shape
        H, two_k = W_att.shape
        k = two_k // 2
        xp = jnp.einsum('bnd,do->bno', x, W_proj)
        xh = xp.reshape(B, N, H, k).transpose(0, 2, 1, 3)
        a_src = jnp.einsum('bhnk,hk->bhn', xh, W_att[:, :k])
        a_dst = jnp.einsum('bhnk,hk->bhn', xh, W_att[:, k:])
        scores = a_src[:, :, :, None] + a_dst[:, :, None, :] + b_att[None, :, None, None]
        scores = jax.nn.leaky_relu(scores, negative_slope=NEG_SLOPE)
        mask = (A > 0)[:, None, :, :]
        scores = jnp.where(mask, scores, NEG_INF)
        att = jax.nn.softmax(scores, axis=-1)
        out = jax.nn.relu(jnp.einsum('bhij,bhjk->bhik', att, xh))
        return out.transpose(0, 2, 1, 3).reshape(B, N, H * k)
    x = _layernorm(x + _L0_gnn_ref(x, adj, L0_gnn_attn_w, L0_gnn_attn_b, L0_gnn_W1, L0_gnn_b1, L0_gnn_W2, L0_gnn_b2, L0_gnn_g1, L0_gnn_beta1, L0_gnn_g2, L0_gnn_beta2), axis=-1)
    x = _layernorm(x + _L1_gnn_ref(x, adj, L1_gnn_W_proj, L1_gnn_W_att, L1_gnn_b_att), axis=-1)
    return x

_drawn_inputs = setup_inputs


def setup_inputs(seed=0):
    import zlib

    import numpy as np

    out = dict(_drawn_inputs(seed))
    spreads = {'L0_gnn_b1': (0.0, 0.1),
     'L0_gnn_b2': (0.0, 0.1),
     'L0_gnn_g1': (1.0, 0.2),
     'L0_gnn_beta1': (0.0, 0.1),
     'L0_gnn_g2': (1.0, 0.2),
     'L0_gnn_beta2': (0.0, 0.1)}
    factors = {'L0_gnn_attn_b': 64.0, 'L1_gnn_b_att': 64.0}
    for name, (base, spread) in spreads.items():
        noise = np.random.default_rng([zlib.crc32(name.encode()), seed]).standard_normal(out[name].shape)
        drawn = base * np.exp(spread * noise) if base else spread * noise
        out[name] = jnp.asarray(drawn.astype(out[name].dtype))
    for name, factor in factors.items():
        out[name] = (out[name] * factor).astype(out[name].dtype)
    return out
```

```python
from contextlib import ExitStack

import concourse.bass as bass
from concourse import mybir

F32 = mybir.dt.float32
BF16 = mybir.dt.bfloat16
I32 = mybir.dt.int32
ALU = mybir.AluOpType
ACT = mybir.ActivationFunctionType
AX = mybir.AxisListType

RMAX = bass.bass_isa.ReduceOp.max

P = 128
GRAPHS, N, D = 16, 512, 256
LAYERS, FF, HEADS, HD = 3, 1024, 8, 32
T = N // P
DT = D // P
FT = FF // P
PAIRS = GRAPHS // 2
SLOTS = 2 * LAYERS
EPS = 1e-5
SLOPE = 0.2
BIG = float(2 ** 100)
HEADS_IN_SLOT = [3, 3, 2, 3, 3, 2]
FFN_BANKS = 3
USES = 2 + FT + T
UNITS = SLOTS + 2 * HEADS
DVE_STEPS = SLOTS * (2 + 3 + 1 + 1 + 3 + T) + 2 * HEADS * 3 + 2 * (1 + 2 + 4) + 2 * (3 + 1 + 2)
COLS = LAYERS * (2 * DT + FT)
CONSTS = 13

GAIN = dict(
    trow=UNITS, ttr=UNITS, rcol=UNITS, rrow=2 * UNITS, exp=2 * UNITS, max=2 * UNITS, prob=2 * UNITS,
    av0=SLOTS * T, av0e=SLOTS * T, hT=SLOTS * DT, hTe=SLOTS * DT, ff1=SLOTS * FT, gelu=SLOTS * FT,
    ff2=SLOTS * T, ff2e=SLOTS * T, hn=SLOTS, hres=SLOTS, x=SLOTS, st=SLOTS,
    av1=2 * HEADS, av1e=2 * HEADS, x1T=2 * DT, x1Te=2 * DT, proj=2 * T, xpe=2 * T,
    tneg=2, tall=2, mprep=2, mT=2 * T, mTe=2 * T, x1=2, out=2, ve=2 * SLOTS + 4, rstd=2 * SLOTS + 4, hmul=SLOTS,
    xin0=16, xin1=16, x0r=32, adj=32, l1ld=96, scrn=32, scrt=32, scrx=32, outst=32, dch=DVE_STEPS,
)


class Counts:

    def __init__(self):
        self.n, self.turn, self.value = dict.fromkeys(GAIN, 0), None, 0

    def skip(self, name, k=1):
        self.n[name] += k

    def __call__(self, name, k=1):
        self.n[name] += k
        return self.n[name] if self.turn is None else self.turn * GAIN[name] + self.n[name]

    def due(self, name, k=1, count=True):
        self.value = self(name, k)
        n = self.n[name]
        if not count:
            self.n[name] -= k
        return self.turn is not None or n > 0


def pairs(eng, c, body):
    body(0)
    before = dict(c.n)
    with eng.Fori(0, PAIRS - 2) as turn:
        c.turn = turn
        body(turn + 1)
        c.turn = None
    for name, n in c.n.items():
        if n != before[name]:
            assert n - before[name] == GAIN[name], (name, n - before[name], GAIN[name])
            c.n[name] = n + (PAIRS - 3) * GAIN[name]
    body(PAIRS - 1)


def slot_of(k):
    nxt = (k + 1) % SLOTS
    return (k % 2, k // 2), (nxt % 2, nxt // 2)


def heads_of(k, l1):
    if not l1:
        return []
    first = sum(HEADS_IN_SLOT[:k])
    return [((first + i) // HEADS, (first + i) % HEADS) for i in range(HEADS_IN_SLOT[k])]


def build(nc, x, adj, attn_w, attn_b, w1, b1, w2, b2, g1, beta1, g2, beta2, w_proj, w_att, b_att, out,
          scr_n, scr_t, scr_x):
    ctx = ExitStack()
    with ctx:
        def sb(name, shape, dt=F32):
            return ctx.enter_context(nc.sbuf_tensor(name, shape, dt))

        def pb(name, shape, dt=F32):
            return ctx.enter_context(nc.psum_tensor(name, shape, dt))

        w1_sb = sb("w1_sb", [P, LAYERS, DT, FF])
        w2_sb = sb("w2_sb", [P, LAYERS, FT, D])
        wp_sb = sb("wp_sb", [P, DT, D + 2 * HEADS])
        col_rows = sb("col_rows", [COLS, P])
        cols = sb("cols", [P, COLS])
        g1_col = cols[:, 0:LAYERS * DT].rearrange("p (l t) -> p l t", l=LAYERS)
        be1_col = cols[:, LAYERS * DT:2 * LAYERS * DT].rearrange("p (l t) -> p l t", l=LAYERS)
        b1_col = cols[:, 2 * LAYERS * DT:].rearrange("p (l t) -> p l t", l=LAYERS)
        g1_row = sb("g1_row", [P, LAYERS, D])
        be1_row = sb("be1_row", [P, LAYERS, D])
        g2_row = sb("g2_row", [P, LAYERS, D])
        be2_row = sb("be2_row", [P, LAYERS, D])
        aw_row = sb("aw_row", [P, LAYERS, 2, D])
        ab_row = sb("ab_row", [P, LAYERS])
        ba_row = sb("ba_row", [P, HEADS])
        ident = sb("ident", [P, P])
        ident_b = sb("ident_b", [P, P], BF16)
        mhalf = sb("mhalf", [P, T])
        xin = [sb(f"xin{s}", [P, T, D + 1]) for s in range(2)]
        xs = [sb(f"xs{s}", [P, T, D + 1]) for s in range(2)]
        mask_n = [sb(f"mask_n{s}", [P, T, N], BF16) for s in range(2)]
        mask_t = [sb(f"mask_t{s}", [P, T, N], BF16) for s in range(2)]
        hT = sb("hT", [P, DT, N])
        G = sb("G", [P, FT, N])
        y_att = sb("y_att", [P, T, D])
        y_ffn = sb("y_ffn", [P, T, D])
        x0r = sb("x0r", [P, T, D])
        x1b = sb("x1b", [P, T, D])
        adj_sb = sb("adj_sb", [P, T, N], I32)
        m0 = sb("m0", [P, T, N], BF16)
        m1 = sb("m1", [P, T, N], BF16)
        dge = sb("dge", [P, T, P], BF16)
        t1_tmp = sb("t1_tmp", [P, T, N], BF16)
        l1n = sb("l1n", [P, T, N], BF16)
        l1t = sb("l1t", [P, T, N], BF16)
        l1x = sb("l1x", [P, T, D])
        xp = sb("xp", [P, T, HEADS, HD + 1])
        o1 = sb("o1", [P, T, D])
        outb = sb("outb", [P, T, D])
        prob = [sb(f"prob{k}", [P, T, N]) for k in range(2)]
        e2 = sb("e2", [P, 2, T // 2, N])
        junk = sb("junk", [P, T, N], BF16)
        junk2 = junk[:].rearrange("p t (a d) -> p t a d", a=2)
        raw0 = sb("raw0", [P, 2, T])
        col0 = sb("col0", [P, 2, T])
        raw1 = sb("raw1", [P, T, 2 * HEADS])
        s1 = sb("s1", [P, T, HEADS])
        t12 = sb("t12", [P, T, HEADS])
        tneg = sb("tneg", [P, HEADS])
        tall = sb("tall", [P, HEADS])
        tmin = sb("tmin", [P, HEADS])
        mx = sb("mx", [P, T])
        z = sb("z", [P, T])
        mrow = sb("mrow", [P, T])
        rcol = [sb(f"rcol{k}", [P, 2, T]) for k in range(2)]
        rec = sb("rec", [P, T])
        rmax = sb("rmax", [P, T])
        stats = sb("stats", [P, T, 6])
        mv = sb("mv", [P, T, 2])
        veps = sb("veps", [P, T])
        rstd = sb("rstd", [P, T])

        ffn = [pb(f"ffn{i}", [P, N]) for i in range(FFN_BANKS)]
        trow = pb("trow", [P, N])
        rrow = [pb(f"rrow{i}", [P, N]) for i in range(2)]
        av0 = pb("av0", [P, N])
        av1 = pb("av1", [P, N])
        mT_ps = av0[:, :].bitcast(BF16).rearrange("p (m t i) -> p m t i", m=2, t=T)
        av1_h = av1[:, 0:T * (HD + 1)].rearrange("p (t k) -> p t k", t=T)
        x1T = prob[1][:, 0:DT, :]

        def sem(name):
            return ctx.enter_context(nc.semaphore(name))

        s_const, s_wts, s_setup, s_init, s_idn = sem("const"), sem("wts"), sem("setup"), sem("init"), sem("idn")
        s_colT, s_cols = sem("colT"), sem("cols")
        s_xin = [sem("xin0"), sem("xin1")]
        s_x0r, s_adj, s_l1ld = sem("x0r"), sem("adj"), sem("l1ld")
        s_scrn, s_scrt, s_scrx, s_outst = sem("scrn"), sem("scrt"), sem("scrx"), sem("outst")
        s_mprep, s_mT, s_mTe = sem("mprep"), sem("mT"), sem("mTe")
        s_st, s_trow, s_ttr, s_rcol, s_rrow = sem("st"), sem("trow"), sem("ttr"), sem("rcol"), sem("rrow")
        s_exp, s_max, s_prob = sem("exp"), sem("max"), sem("prob")
        s_av0, s_av0e, s_av1, s_av1e = sem("av0"), sem("av0e"), sem("av1"), sem("av1e")
        s_ve, s_rstd = sem("ve"), sem("rstd")
        s_hn, s_hT, s_hTe, s_ff1, s_gelu = sem("hn"), sem("hT"), sem("hTe"), sem("ff1"), sem("gelu")
        s_ff2, s_ff2e, s_hmul, s_hres, s_x = sem("ff2"), sem("ff2e"), sem("hmul"), sem("hres"), sem("x")
        s_x1T, s_x1Te, s_proj, s_xpe = sem("x1T"), sem("x1Te"), sem("proj"), sem("xpe")
        s_tneg, s_tall = sem("tneg"), sem("tall")
        s_x1, s_out = sem("x1"), sem("out")
        s_dch = sem("dch")
        s_passed = sem("passed")
        block = ctx.enter_context(nc.Block())

        def ffn_bank(k, use):
            return ffn[(k * USES + use) % FFN_BANKS]

        def nodes(dram, p, s):
            return dram.rearrange("(g s) (t p) d -> g s p t d", s=2, p=P)[p, s]

        def flat(dram, p, s):
            return dram.rearrange("(g s) p n -> g s p n", s=2)[p, s]

        def is_turn(p, n):
            return isinstance(p, int) and p == n

        def state(s, l):
            return xin[s] if l == 0 else xs[s]

        def rows(table, l):
            return table[:, l, :].unsqueeze(1).broadcast_to([P, T, D])

        @block.sync
        def _(sp):
            c = Counts()

            def load_x(p, s):
                sp.dma_start(xin[s][:, :, 0:D], nodes(x, p, s)).then_inc(s_xin[s], 16)

            def load_adj(p, s):
                sp.dma_start(adj_sb[:], nodes(adj, p, s)).then_inc(s_adj, 16)

            def load_x0(p, s):
                sp.dma_start(x0r[:], nodes(x, p, s)).then_inc(s_x0r, 16)

            def bcast(dst, src):
                sp.dma_start(dst, src.partition_broadcast(P)).then_inc(s_const, 16)

            def rows_in(src, at, n):
                column(col_rows[at:at + n, :], src.rearrange("l (t p) -> (l t) p", p=P))

            def column(dst, src):
                sp.dma_start(dst, src).then_inc(s_const, 16)

            def masks(p, s, then_adj=None):
                sp.wait_ge(s_mprep, c("mprep"))
                sp.sem_inc(s_passed, 1)
                sp.dma_start(flat(scr_n, p, s), mask_n[s][:].rearrange("p t n -> p (t n)")).then_inc(s_scrn, 16)
                if then_adj is not None:
                    load_adj(*then_adj)
                sp.wait_ge(s_mTe, c("mTe", T))
                sp.sem_inc(s_passed, 1)
                sp.dma_start(flat(scr_t, p, s), t1_tmp[:].rearrange("p t n -> p (t n)")).then_inc(s_scrt, 16)

            def store_x1(p, s):
                sp.wait_ge(s_x1, c("x1"))
                sp.sem_inc(s_passed, 1)
                sp.dma_start(flat(scr_x, p, s), x1b[:].rearrange("p t d -> p (t d)")).then_inc(s_scrx, 16)

            def load_l1(p, s, sent=True):
                if s == 0 and sent:
                    sp.wait_ge(s_scrn, c("scrn", 32))
                    sp.sem_inc(s_passed, 1)
                    sp.wait_ge(s_scrt, c("scrt", 32))
                    sp.sem_inc(s_passed, 1)
                sp.wait_ge(s_scrx, c("scrx", 16))
                sp.sem_inc(s_passed, 1)
                sp.dma_start(l1n[:].rearrange("p t n -> p (t n)"), flat(scr_n, p, s)).then_inc(s_l1ld, 16)
                sp.dma_start(l1t[:].rearrange("p t n -> p (t n)"), flat(scr_t, p, s)).then_inc(s_l1ld, 16)
                sp.dma_start(l1x[:].rearrange("p t d -> p (t d)"), flat(scr_x, p, s)).then_inc(s_l1ld, 16)

            def store_out(p, s):
                sp.wait_ge(s_out, c("out"))
                sp.sem_inc(s_passed, 1)
                sp.dma_start(nodes(out, p, s), outb[:]).then_inc(s_outst, 16)

            load_adj(0, 0)
            load_x(0, 0)
            bcast(aw_row[:].rearrange("p l a d -> p (l a d)"), attn_w.rearrange("l d -> (l d)"))
            bcast(ab_row[:], attn_b)
            bcast(g1_row[:].rearrange("p l d -> p (l d)"), g1.rearrange("l d -> (l d)"))
            bcast(be1_row[:].rearrange("p l d -> p (l d)"), beta1.rearrange("l d -> (l d)"))
            bcast(g2_row[:].rearrange("p l d -> p (l d)"), g2.rearrange("l d -> (l d)"))
            bcast(be2_row[:].rearrange("p l d -> p (l d)"), beta2.rearrange("l d -> (l d)"))
            bcast(y_ffn[:, 0:LAYERS, :].rearrange("p l d -> p (l d)"), b2.rearrange("l d -> (l d)"))
            bcast(o1[:, 0:2, :].rearrange("p l d -> p (l d)"), w_att.rearrange("l d -> (l d)"))
            bcast(ba_row[:], b_att)
            rows_in(g1, 0, LAYERS * DT)
            rows_in(beta1, LAYERS * DT, LAYERS * DT)
            rows_in(b1, 2 * LAYERS * DT, LAYERS * FT)
            column(wp_sb[:, :, 0:D], w_proj.rearrange("(t p) o -> p t o", p=P))
            for l in range(LAYERS):
                sp.dma_start(w1_sb[:, l], w1[l].rearrange("(t p) f -> p t f", p=P)).then_inc(s_wts, 16)
                sp.dma_start(w2_sb[:, l], w2[l].rearrange("(t p) f -> p t f", p=P)).then_inc(s_wts, 16)
            load_x(0, 1)
            masks(0, 0, then_adj=(0, 1))
            masks(0, 1)
            sp.wait_ge(s_av0e, c("av0e", T))
            sp.sem_inc(s_passed, 1)
            c.skip("scrn", 32)
            c.skip("scrt", 32)

            def body(p):
                first, last = is_turn(p, 0), is_turn(p, PAIRS - 1)
                if not last:
                    load_adj(p + 1, 0)
                    load_x(p + 1, 0)
                if not first:
                    load_l1(p - 1, 0)
                    store_x1(p - 1, 1)
                load_x0(p, 0)
                sp.wait_ge(s_av0e, c("av0e", T))
                sp.sem_inc(s_passed, 1)
                if not last:
                    load_x(p + 1, 1)
                c.skip("av0e", (SLOTS - 1) * T)
                if not first:
                    store_out(p - 1, 0)
                    load_l1(p - 1, 1)
                if not last:
                    masks(p + 1, 0, then_adj=(p + 1, 1))
                store_x1(p, 0)
                load_x0(p, 1)
                if not first:
                    store_out(p - 1, 1)
                if not last:
                    masks(p + 1, 1)

            pairs(sp, c, body)
            load_l1(PAIRS - 1, 0, sent=False)
            store_x1(PAIRS - 1, 1)
            store_out(PAIRS - 1, 0)
            load_l1(PAIRS - 1, 1)
            store_out(PAIRS - 1, 1)
            sp.wait_ge(s_outst, 16 * GRAPHS)
            sp.wait_ge(s_scrn, 16 * GRAPHS)
            sp.wait_ge(s_scrt, 16 * GRAPHS)
            sp.wait_ge(s_scrx, 16 * GRAPHS)

        @block.gpsimd
        def _(pool):
            c = Counts()
            nc.gpsimd.memset(ident[:], 0.0).then_inc(s_idn, 1)
            nc.gpsimd.memset(ident_b[:], 0.0).then_inc(s_idn, 1)
            nc.gpsimd.memset(mhalf[:], -0.5).then_inc(s_idn, 1)
            pool.wait_ge(s_idn, 3)
            for m in (ident, ident_b):
                nc.gpsimd.affine_select(out=m[:], in_=m[:], compare_op=ALU.not_equal, fill=1.0, base=0,
                                        pattern=[[-1, P]], channel_multiplier=1).then_inc(s_idn, 1)
            pool.wait_ge(s_const, 16 * CONSTS)
            pool.wait_ge(s_setup, 1)

            def inverse_deviation():
                pool.wait_ge(s_ve, c("ve"))
                nc.gpsimd.tensor_tensor(rstd[:], veps[:], mhalf[:], ALU.pow).then_inc(s_rstd, 1)

            def residual(s, l):
                h = xs[s][:, :, 0:D]
                pool.wait_ge(s_hT, c("hT", DT))
                nc.gpsimd.tensor_tensor(h, h, rows(g1_row, l), ALU.mult).then_inc(s_hmul, 1)
                pool.wait_ge(s_hmul, c("hmul"))
                nc.gpsimd.tensor_tensor(h, h, rows(be1_row, l), ALU.add).then_inc(s_hres, 1)

            def least_targets():
                pool.wait_ge(s_tneg, c("tneg"))
                pool.sem_inc(s_passed, 1)
                nc.gpsimd.partition_all_reduce(tall[:], tneg[:], P, RMAX).then_inc(s_tall, 1)

            def finish(l):
                inverse_deviation()
                if l == LAYERS - 1:
                    inverse_deviation()

            inverse_deviation()

            def body(p):
                first, last = is_turn(p, 0), is_turn(p, PAIRS - 1)
                for k in range(SLOTS):
                    (s, l), (s2, l2) = slot_of(k)
                    if not (first and k == 0):
                        finish((k - 1) % SLOTS // 2)
                    residual(s, l)
                    if k in (0, 3) and not first:
                        least_targets()
                    if not (last and k == SLOTS - 1):
                        inverse_deviation()
                    if k in (2, 5) and not first:
                        inverse_deviation()

            pairs(pool, c, body)
            finish(LAYERS - 1)
            for s in range(2):
                least_targets()
                inverse_deviation()

        @block.scalar
        def _(act):
            c = Counts()
            c.skip("max", -2)
            c.skip("av0", -T)
            c.skip("av1", -1)
            c.skip("scrt", -16)
            act.wait_ge(s_colT, 1)
            nc.scalar.copy(cols[:], ffn[0][:, 0:COLS]).then_inc(s_cols, 1)
            act.wait_ge(s_cols, 1)

            def exps(kind, head=None):
                if kind == 0:
                    if c.due("av0", T):
                        act.wait_ge(s_av0, c.value)
                    t, t2 = raw0[:, 1, :], col0[:, 1, :]
                else:
                    if c.due("av1"):
                        act.wait_ge(s_av1, c.value)
                    t, t2 = raw1[:, :, HEADS + head], t12[:, :, head]
                for half in range(2):
                    tiles = range(half * T // 2, (half + 1) * T // 2)
                    if half == 0:
                        act.wait_ge(s_rrow, c("rrow"))
                    for j in tiles:
                        nc.scalar.activation(prob[kind][:, j, :], rrow[0][:], ACT.Exp, bias=t[:, j:j + 1])
                    if half == 0:
                        act.wait_ge(s_rrow, c("rrow"))
                    if c.due("max"):
                        act.wait_ge(s_max, c.value)
                    for j in tiles:
                        last = nc.scalar.activation(e2[:, half, j % 2, :], rrow[1][:], ACT.Exp, bias=t2[:, j:j + 1])
                    last.then_inc(s_exp, 1)

            def transposed(k, dt, l):
                act.wait_ge(s_hT, c("hT"))
                nc.scalar.activation(hT[:, dt, :], ffn_bank(k, dt)[:], ACT.Identity, bias=be1_col[:, l, dt:dt + 1],
                                     scale=g1_col[:, l, dt:dt + 1]).then_inc(s_hTe, 1)

            def gelu(k, l, f):
                act.wait_ge(s_ff1, c("ff1"))
                nc.scalar.activation(G[:, f, :], ffn_bank(k, 2 + f)[:], ACT.Gelu,
                                     bias=b1_col[:, l, f:f + 1]).then_inc(s_gelu, 1)

            def masks(s):
                if c.due("scrt", 16):
                    act.wait_ge(s_scrt, c.value)
                for i in range(T):
                    act.wait_ge(s_mT, c("mT"))
                    nc.scalar.copy(mask_t[s][:, :, i * P:(i + 1) * P], mT_ps[:, 0])
                    nc.scalar.copy(t1_tmp[:, :, i * P:(i + 1) * P], mT_ps[:, 1]).then_inc(s_mTe, 1)

            def state_out(dt):
                if dt == 0:
                    if c.due("av1", count=False):
                        act.wait_ge(s_av1, c.value)
                act.wait_ge(s_x1T, c("x1T"))
                nc.scalar.copy(x1T[:, dt, :], av1[:]).then_inc(s_x1Te, 1)

            def values_out(t):
                act.wait_ge(s_proj, c("proj"))
                nc.scalar.copy(xp[:, t, :, 0:HD], av1[:, 0:D].rearrange("p (h k) -> p h k", h=HEADS))
                nc.scalar.copy(raw1[:, t, :], av1[:, D:D + 2 * HEADS]).then_inc(s_xpe, 1)

            def graph_begins():
                for dt in range(DT):
                    state_out(dt)
                for t in range(T):
                    values_out(t)

            masks(0)
            masks(1)
            exps(0)

            def body(p):
                first, last = is_turn(p, 0), is_turn(p, PAIRS - 1)
                for k in range(SLOTS):
                    (s, l), (s2, l2) = slot_of(k)
                    for dt in range(DT):
                        transposed(k, dt, l)
                    for f in range(FT):
                        if not first and k in (0, 3):
                            if f < DT:
                                state_out(f)
                            elif f < DT + T:
                                values_out(f - DT)
                        gelu(k, l, f)
                    if not (last and k == SLOTS - 1):
                        exps(0)
                    for _, head in heads_of(k, not first):
                        exps(1, head)
                    if not last and k in (4, 5):
                        masks(k - 4)

            pairs(act, c, body)
            for s in range(2):
                graph_begins()
                for head in range(HEADS):
                    exps(1, head)

        @block.vector
        def _(dve):
            c = Counts()
            c.skip("scrx", -16)
            c.skip("scrn", -32)
            c.skip("outst", -16)
            v = nc.vector

            def norm(src, dst, done):
                for t in range(T):
                    last = v.bn_stats(stats[:, t, :], src[:, t, 0:D])
                last.then_inc(s_dch, 1)
                dve.wait_ge(s_dch, c("dch"))
                dve.sem_inc(s_passed, 1)
                for t in range(T):
                    last = v.bn_aggr(mv[:, t, :], stats[:, t, :])
                last.then_inc(s_dch, 1)
                dve.wait_ge(s_dch, c("dch"))
                v.tensor_scalar_add(veps[:], mv[:, :, 1], EPS).then_inc(s_ve, 1)
                dve.wait_ge(s_rstd, c("rstd"))
                for t in range(T):
                    last = v.tensor_scalar(dst[:, t, 0:D], src[:, t, 0:D], mv[:, t, 0:1], rstd[:, t:t + 1],
                                           ALU.subtract, ALU.mult)
                last.then_inc(done, 1)

            def make_masks(s):
                dve.wait_ge(s_adj, c("adj", 16))
                if c.due("scrn", 16):
                    dve.wait_ge(s_scrn, c.value)
                v.tensor_scalar(m0[:], adj_sb[:], 0.0, None, ALU.is_gt).then_inc(s_dch, 1)
                dve.wait_ge(s_dch, c("dch"))
                v.tensor_scalar(mask_n[s][:], m0[:], -1.0, BIG, ALU.add, ALU.mult)
                v.tensor_reduce(rmax[:], m0[:], AX.X, ALU.max).then_inc(s_dch, 1)
                dve.wait_ge(s_dch, c("dch"))
                v.tensor_scalar(rmax[:], rmax[:], 0.0, None, ALU.is_le).then_inc(s_dch, 1)
                dve.wait_ge(s_dch, c("dch"))
                for t in range(T):
                    v.tensor_scalar(m1[:, t, :], m0[:, t, :], rmax[:, t:t + 1], None, ALU.max)
                for t in range(T):
                    last = v.scalar_tensor_tensor(dge[:, t, :], adj_sb[:, t, t * P:(t + 1) * P], 0.0, ident_b[:],
                                                  ALU.is_ge, ALU.mult)
                last.then_inc(s_dch, 1)
                dve.wait_ge(s_dch, c("dch"))
                for t in range(T):
                    last = v.tensor_tensor(m0[:, t, t * P:(t + 1) * P], m0[:, t, t * P:(t + 1) * P], dge[:, t, :],
                                           ALU.max)
                last.then_inc(s_mprep, 1)

            def scores(s, l):
                if l == 0:
                    dve.wait_ge(s_xin[s], c(f"xin{s}", 16))
                for a in range(2):
                    for t in range(T):
                        last = v.tensor_tensor_reduce(out=junk2[:, t, a, :], in0=state(s, l)[:, t, 0:D], in1=aw_row[:, l, a, :],
                                                      scale=1.0, scalar=0.0, op0=ALU.mult, op1=ALU.add,
                                                      accum_out=raw0[:, a, t:t + 1])
                last.then_inc(s_st, 1)
                dve.wait_ge(s_st, c("st"))
                v.tensor_scalar(col0[:, 0, :], raw0[:, 0, :], ab_row[:, l:l + 1], None, ALU.add)
                v.tensor_scalar(col0[:, 1, :], raw0[:, 1, :], SLOPE, None, ALU.mult).then_inc(s_dch, 1)
                dve.wait_ge(s_dch, c("dch"))

            def row_maxima(kind, s=None, head=None):
                mask = mask_n[s] if kind == 0 else l1n
                src = col0[:, 0, :] if kind == 0 else s1[:, :, head]
                least = -3.0e38 if kind == 0 else tmin[:, head:head + 1]
                dve.wait_ge(s_trow, c("trow"))
                dve.sem_inc(s_passed, 1)
                for t in range(T):
                    last = v.tensor_tensor_reduce(out=junk[:, t, :], in0=trow[:], in1=mask[:, t, :], scale=1.0,
                                                  scalar=least, op0=ALU.add, op1=ALU.max, accum_out=mx[:, t:t + 1])
                last.then_inc(s_ttr, 1)
                dve.wait_ge(s_ttr, c("ttr"))
                if kind == 0:
                    v.tensor_tensor(mx[:], mx[:], raw0[:, 1, :], ALU.max).then_inc(s_dch, 1)
                    dve.wait_ge(s_dch, c("dch"))
                v.tensor_tensor(z[:], mx[:], src, ALU.add).then_inc(s_dch, 1)
                dve.wait_ge(s_dch, c("dch"))
                v.scalar_tensor_tensor(mrow[:], z[:], SLOPE, z[:], ALU.mult, ALU.max).then_inc(s_dch, 1)
                dve.wait_ge(s_dch, c("dch"))
                v.tensor_tensor(rcol[kind][:, 0, :], src, mrow[:], ALU.subtract)
                v.scalar_tensor_tensor(rcol[kind][:, 1, :], src, SLOPE, mrow[:], ALU.mult,
                                       ALU.subtract).then_inc(s_rcol, 1)

            def combine(kind, s=None):
                mask = mask_t[s] if kind == 0 else l1t
                for half in range(2):
                    j = slice(half * T // 2, (half + 1) * T // 2)
                    dve.wait_ge(s_exp, c("exp"))
                    v.tensor_tensor(prob[kind][:, j, :], prob[kind][:, j, :], e2[:, half], ALU.max).then_inc(s_max, 1)
                    dve.wait_ge(s_max, c("max"))
                    v.tensor_tensor(prob[kind][:, j, :], prob[kind][:, j, :], mask[:, j, :], ALU.min).then_inc(s_prob, 1)

            def attended(s, l, t):
                dve.wait_ge(s_av0, c("av0"))
                v.reciprocal(rec[:, 0:1], av0[:, D:D + 1]).then_inc(s_dch, 1)
                dve.wait_ge(s_dch, c("dch"))
                v.scalar_tensor_tensor(y_att[:, t, :], av0[:, 0:D], rec[:, 0:1], state(s, l)[:, t, 0:D], ALU.mult,
                                       ALU.add).then_inc(s_av0e, 1)

            def norm_attended(s):
                dve.wait_ge(s_av0e, c("av0e", T))
                norm(y_att, xs[s], s_hn)

            def fed_forward(k, s, t):
                if t == 0:
                    dve.wait_ge(s_hres, c("hres"))
                dve.wait_ge(s_ff2, c("ff2"))
                v.tensor_tensor(y_ffn[:, t, :], ffn_bank(k, 2 + FT + t)[:, 0:D], xs[s][:, t, 0:D],
                                ALU.add).then_inc(s_ff2e, 1)

            def layer_ends(s, l):
                dve.wait_ge(s_ff2e, c("ff2e", T))
                norm(y_ffn, y_ffn, s_dch)
                dve.wait_ge(s_dch, c("dch"))
                v.tensor_tensor(y_ffn[:], y_ffn[:], rows(g2_row, l), ALU.mult).then_inc(s_dch, 1)
                dve.wait_ge(s_dch, c("dch"))
                v.tensor_tensor(xs[s][:, :, 0:D], y_ffn[:], rows(be2_row, l), ALU.add).then_inc(s_x, 1)
                dve.wait_ge(s_x, c("x"))
                if l == LAYERS - 1:
                    dve.wait_ge(s_x0r, c("x0r", 16))
                    v.tensor_tensor(y_ffn[:], xs[s][:, :, 0:D], x0r[:], ALU.add).then_inc(s_dch, 1)
                    dve.wait_ge(s_dch, c("dch"))
                    if c.due("scrx", 16):
                        dve.wait_ge(s_scrx, c.value)
                    norm(y_ffn, x1b, s_x1)

            def graph_begins():
                dve.wait_ge(s_l1ld, c("l1ld", 48))
                dve.wait_ge(s_xpe, c("xpe", T))
                v.tensor_tensor(s1[:], raw1[:, :, 0:HEADS], ba_row[:].unsqueeze(1).broadcast_to([P, T, HEADS]),
                                ALU.add).then_inc(s_dch, 1)
                dve.wait_ge(s_dch, c("dch"))
                v.tensor_scalar(t12[:], raw1[:, :, HEADS:], SLOPE, None, ALU.mult)
                v.tensor_reduce(tmin[:], raw1[:, :, HEADS:].rearrange("p t h -> p h t"), AX.X, ALU.min).then_inc(s_dch, 1)
                dve.wait_ge(s_dch, c("dch"))
                v.tensor_scalar(tneg[:], tmin[:], -1.0, None, ALU.mult).then_inc(s_tneg, 1)
                dve.wait_ge(s_tall, c("tall"))
                v.tensor_scalar(tmin[:], tall[:], -1.0, None, ALU.mult).then_inc(s_dch, 1)
                dve.wait_ge(s_dch, c("dch"))

            def head_out(head):
                dve.wait_ge(s_av1, c("av1"))
                v.reciprocal(rec[:], av1_h[:, :, HD]).then_inc(s_dch, 1)
                dve.wait_ge(s_dch, c("dch"))
                v.tensor_tensor(o1[:, :, head * HD:(head + 1) * HD], av1_h[:, :, 0:HD],
                                rec[:].unsqueeze(2).broadcast_to([P, T, HD]), ALU.mult).then_inc(s_av1e, 1)

            def graph_ends():
                dve.wait_ge(s_av1e, c("av1e", HEADS))
                v.scalar_tensor_tensor(o1[:], o1[:], 0.0, l1x[:], ALU.max, ALU.add).then_inc(s_dch, 1)
                dve.wait_ge(s_dch, c("dch"))
                if c.due("outst", 16):
                    dve.wait_ge(s_outst, c.value)
                norm(o1, outb, s_out)

            for b in xin + xs:
                v.memset(b[:, :, D:D + 1], 1.0)
            v.memset(xp[:, :, :, HD:HD + 1], 1.0).then_inc(s_init, 1)
            dve.wait_ge(s_idn, 5)
            make_masks(0)
            dve.wait_ge(s_const, 16 * CONSTS)
            watt = o1[:, 0:2, :].rearrange("p a d -> p (a d)").rearrange("p (h a k) -> p h a k", h=HEADS, a=2)
            prod = y_att[:, 0, :].rearrange("p (h k) -> p h k", h=HEADS)
            for dt in range(DT):
                for a in range(2):
                    v.tensor_tensor(prod, wp_sb[:, dt, 0:D].rearrange("p (h k) -> p h k", h=HEADS),
                                    watt[:, :, a, :], ALU.mult).then_inc(s_dch, 1)
                    dve.wait_ge(s_dch, c("dch"))
                    v.tensor_reduce(wp_sb[:, dt, D + a * HEADS:D + (a + 1) * HEADS], prod, AX.X, ALU.add).then_inc(s_dch, 1)
                    dve.wait_ge(s_dch, c("dch"))
            v.tensor_tensor(be1_row[:], be1_row[:], y_ffn[:, 0:LAYERS, :], ALU.add).then_inc(s_setup, 1)
            scores(0, 0)
            row_maxima(0, 0)
            make_masks(1)
            dve.wait_ge(s_mTe, c("mTe", T))
            combine(0, 0)
            for t in range(T):
                attended(0, 0, t)
            norm_attended(0)

            def body(p):
                first, last = is_turn(p, 0), is_turn(p, PAIRS - 1)
                for k in range(SLOTS):
                    (s, l), (s2, l2) = slot_of(k)
                    heads = heads_of(k, not first)
                    att = not (last and k == SLOTS - 1)
                    if not (first and k == 0):
                        layer_ends(1 - s, (k - 1) % SLOTS // 2)
                    if att:
                        scores(s2, l2)
                        row_maxima(0, s2)
                    if heads and k in (0, 3):
                        graph_begins()
                    if heads:
                        row_maxima(1, head=heads[0][1])
                    if att:
                        if l2 == 0:
                            dve.wait_ge(s_mTe, c("mTe", T))
                        combine(0, s2)
                    if heads:
                        row_maxima(1, head=heads[1][1])
                    for t in range(2):
                        fed_forward(k, s, t)
                        if att:
                            attended(s2, l2, 2 * t)
                            attended(s2, l2, 2 * t + 1)
                    if att:
                        norm_attended(s2)
                    if heads:
                        combine(1)
                        if len(heads) > 2:
                            row_maxima(1, head=heads[2][1])
                        head_out(heads[0][1])
                    fed_forward(k, s, 2)
                    if heads:
                        combine(1)
                        head_out(heads[1][1])
                        if len(heads) > 2:
                            combine(1)
                    fed_forward(k, s, 3)
                    if len(heads) > 2:
                        head_out(heads[2][1])
                    if heads and k in (2, 5):
                        graph_ends()
                    if not last and k in (4, 5):
                        make_masks(k - 4)

            pairs(dve, c, body)
            layer_ends(1, LAYERS - 1)
            for s in range(2):
                graph_begins()
                row_maxima(1, head=0)
                for head in range(HEADS):
                    if head + 1 < HEADS:
                        row_maxima(1, head=head + 1)
                    combine(1)
                    head_out(head)
                graph_ends()

        @block.tensor
        def _(pe):
            c = Counts()
            c.skip("ff2e", -3)
            c.skip("ttr", -1)
            c.skip("exp", -2)
            c.skip("av0e", -1)
            c.skip("mTe", -1)
            c.skip("av1e", -1)
            te = nc.tensor

            def spread(row, col):
                for t in range(T):
                    last = te.transpose(row[:, t * P:(t + 1) * P], col[:, t:t + 1].broadcast_to([P, P]), ident[:])
                return last

            def target_row(kind, head=None):
                if kind == 0:
                    pe.wait_ge(s_st, c("st"))
                if c.due("ttr"):
                    pe.wait_ge(s_ttr, c.value)
                spread(trow, raw0[:, 1, :] if kind == 0 else raw1[:, :, HEADS + head]).then_inc(s_trow, 1)

            def exp_rows(kind):
                pe.wait_ge(s_rcol, c("rcol"))
                if c.due("exp", 2):
                    pe.wait_ge(s_exp, c.value)
                for a in range(2):
                    spread(rrow[a], rcol[kind][:, a, :]).then_inc(s_rrow, 1)

            def attend(s, l, t):
                if t == 0:
                    pe.wait_ge(s_prob, c("prob", 2))
                    if c.due("mTe", count=False):
                        pe.wait_ge(s_mTe, c.value)
                    if l == 0:
                        pe.wait_ge(s_xin[s], c(f"xin{s}", 16))
                if c.due("av0e"):
                    pe.wait_ge(s_av0e, c.value)
                for j in range(T):
                    last = te.matmul(av0[:, 0:D + 1], prob[0][:, j, t * P:(t + 1) * P], state(s, l)[:, j, :],
                                     start=j == 0, stop=j == T - 1)
                last.then_inc(s_av0, 1)

            def attend_head(head):
                if head == 0:
                    pe.wait_ge(s_xpe, c("xpe"))
                pe.wait_ge(s_prob, c("prob", 2))
                if c.due("av1e"):
                    pe.wait_ge(s_av1e, c.value)
                for t in range(T):
                    for j in range(T):
                        last = te.matmul(av1_h[:, t, :], prob[1][:, j, t * P:(t + 1) * P], xp[:, j, head, :],
                                         start=j == 0, stop=j == T - 1)
                last.then_inc(s_av1, 1)

            def transpose_state(k, s, dt):
                if dt == 0:
                    pe.wait_ge(s_hn, c("hn"))
                if c.due("ff2e"):
                    pe.wait_ge(s_ff2e, c.value)
                for t in range(T):
                    last = te.transpose(ffn_bank(k, dt)[:, t * P:(t + 1) * P], xs[s][:, t, dt * P:(dt + 1) * P], ident[:])
                last.then_inc(s_hT, 1)

            def first_product(k, l, f):
                if f == 0:
                    if c.due("ff2e"):
                        pe.wait_ge(s_ff2e, c.value)
                    pe.wait_ge(s_hTe, c("hTe", DT))
                if f >= FFN_BANKS:
                    pe.wait_ge(s_gelu, c("gelu"))
                for dt in range(DT):
                    last = te.matmul(ffn_bank(k, 2 + f)[:], w1_sb[:, l, dt, f * P:(f + 1) * P], hT[:, dt, :],
                                     start=dt == 0, stop=dt == DT - 1)
                last.then_inc(s_ff1, 1)

            def second_product(k, l, t):
                if t == 0:
                    pe.wait_ge(s_gelu, c("gelu", FFN_BANKS))
                if t == FFN_BANKS:
                    if c.due("ff2e"):
                        pe.wait_ge(s_ff2e, c.value)
                for f in range(FT):
                    last = te.matmul(ffn_bank(k, 2 + FT + t)[:, 0:D], G[:, f, t * P:(t + 1) * P], w2_sb[:, l, f, :],
                                     start=f == 0, stop=f == FT - 1)
                last.then_inc(s_ff2, 1)

            def masks(first):
                pe.wait_ge(s_mprep, c("mprep"))
                for i in range(T):
                    if i == 0:
                        if c.due("av0e", count=False):
                            pe.wait_ge(s_av0e, c.value)
                    if c.due("mTe"):
                        pe.wait_ge(s_mTe, c.value)
                    for m, src in enumerate((m0, m1)):
                        for j in range(T):
                            last = te.transpose(mT_ps[:, m, j, :], src[:, i, j * P:(j + 1) * P], ident_b[:])
                    last.then_inc(s_mT, 1)

            def state_in(dt):
                if dt == 0:
                    pe.wait_ge(s_l1ld, c("l1ld", 48))
                    if c.due("av1e", count=False):
                        pe.wait_ge(s_av1e, c.value)
                else:
                    pe.wait_ge(s_x1Te, c("x1Te"))
                for t in range(T):
                    last = te.transpose(av1[:, t * P:(t + 1) * P], l1x[:, t, dt * P:(dt + 1) * P], ident[:])
                last.then_inc(s_x1T, 1)

            def project(t):
                if t == 0:
                    pe.wait_ge(s_x1Te, c("x1Te"))
                else:
                    pe.wait_ge(s_xpe, c("xpe"))
                for dt in range(DT):
                    last = te.matmul(av1[:, 0:D + 2 * HEADS], x1T[:, dt, t * P:(t + 1) * P], wp_sb[:, dt, :],
                                     start=dt == 0, stop=dt == DT - 1)
                last.then_inc(s_proj, 1)

            pe.wait_ge(s_idn, 5)
            pe.wait_ge(s_init, 1)
            pe.wait_ge(s_const, 16 * CONSTS)
            te.transpose(ffn[0][:, 0:COLS], col_rows[:], ident[0:COLS, 0:COLS]).then_inc(s_colT, 1)
            masks(True)
            target_row(0)
            exp_rows(0)
            masks(False)
            for t in range(T):
                attend(0, 0, t)
            pe.wait_ge(s_cols, 1)
            pe.wait_ge(s_setup, 1)
            pe.wait_ge(s_wts, 16 * 2 * LAYERS)

            def body(p):
                first, last = is_turn(p, 0), is_turn(p, PAIRS - 1)
                for k in range(SLOTS):
                    (s, l), (s2, l2) = slot_of(k)
                    heads = heads_of(k, not first)
                    att = not (last and k == SLOTS - 1)
                    for dt in range(DT):
                        transpose_state(k, s, dt)
                    for f in range(FT):
                        if not first and k in (0, 3):
                            if f < DT:
                                state_in(f)
                            elif f < DT + T:
                                project(f - DT)
                        if f == 6 and att:
                            target_row(0)
                        first_product(k, l, f)
                    if att:
                        exp_rows(0)
                    if heads:
                        if k in (0, 3):
                            if c.due("xpe", count=False):
                                pe.wait_ge(s_xpe, c.value)
                        target_row(1, heads[0][1])
                    second_product(k, l, 0)
                    if heads:
                        exp_rows(1)
                    if att:
                        attend(s2, l2, 0)
                    if heads:
                        target_row(1, heads[1][1])
                    if att:
                        attend(s2, l2, 1)
                    second_product(k, l, 1)
                    if att:
                        attend(s2, l2, 2)
                        attend(s2, l2, 3)
                    if heads:
                        exp_rows(1)
                        attend_head(heads[0][1])
                        if len(heads) > 2:
                            target_row(1, heads[2][1])
                    second_product(k, l, 2)
                    if len(heads) > 2:
                        exp_rows(1)
                    if heads:
                        attend_head(heads[1][1])
                    second_product(k, l, 3)
                    if len(heads) > 2:
                        attend_head(heads[2][1])
                    if not last and k in (4, 5):
                        masks(False)

            pairs(pe, c, body)
            for s in range(2):
                for dt in range(DT):
                    state_in(dt)
                for t in range(T):
                    project(t)
                if c.due("xpe", count=False):
                    pe.wait_ge(s_xpe, c.value)
                target_row(1, 0)
                exp_rows(1)
                for head in range(HEADS):
                    if head + 1 < HEADS:
                        target_row(1, head + 1)
                        exp_rows(1)
                    attend_head(head)


_INS = ["x", "adj", "L0_gnn_attn_w", "L0_gnn_attn_b", "L0_gnn_W1", "L0_gnn_b1", "L0_gnn_W2", "L0_gnn_b2",
        "L0_gnn_g1", "L0_gnn_beta1", "L0_gnn_g2", "L0_gnn_beta2", "L1_gnn_W_proj", "L1_gnn_W_att", "L1_gnn_b_att"]


def kernel(**inputs):
    import numpy as np
    import concourse.bacc as bacc
    from concourse.bass_utils import run_bass_kernel_spmd as run

    nc = bacc.Bacc("TRN2", target_bir_lowering=False, num_devices=1, dynamic_dma_scratch_size=1024)
    arrays, args = {}, []
    for name in _INS:
        a = np.ascontiguousarray(inputs[name])
        arrays[f"in_{name}"] = a
        args.append(nc.dram_tensor(f"in_{name}", a.shape, mybir.dt.from_np(a.dtype), kind="ExternalInput").ap())
    out = nc.dram_tensor("out_0", (GRAPHS, N, D), F32, kind="ExternalOutput").ap()
    scr_n = nc.dram_tensor("scr_n", (GRAPHS, P, T * N), BF16, kind="Internal").ap()
    scr_t = nc.dram_tensor("scr_t", (GRAPHS, P, T * N), BF16, kind="Internal").ap()
    scr_x = nc.dram_tensor("scr_x", (GRAPHS, P, T * D), F32, kind="Internal").ap()
    build(nc, *args, out, scr_n, scr_t, scr_x)
    r = run(nc, [arrays], core_ids=[0])
    return r.results[0]["out_0"]
```

```python
from contextlib import ExitStack

import concourse.bass as bass
from concourse import mybir

F32 = mybir.dt.float32
BF16 = mybir.dt.bfloat16
I32 = mybir.dt.int32
ALU = mybir.AluOpType
ACT = mybir.ActivationFunctionType
AX = mybir.AxisListType

RMAX = bass.bass_isa.ReduceOp.max

P = 128
GRAPHS, N, D = 16, 512, 256
LAYERS, FF, HEADS, HD = 3, 1024, 8, 32
T = N // P
DT = D // P
FT = FF // P
PAIRS = GRAPHS // 2
SLOTS = 2 * LAYERS
EPS = 1e-5
SLOPE = 0.2
BIG = float(2 ** 100)
HEADS_IN_SLOT = [3, 3, 2, 3, 3, 2]
BANKS = 2
PARTS = 2
UNITS = SLOTS + 2 * HEADS
DVE_STEPS = SLOTS * (2 + 3 + 1 + 1 + 2 + T) + 2 * HEADS * 3 + 2 * (1 + 2 + 4) + 2 * (3 + 2)
ATTENDED, RESIDUAL, FED, LAST = range(4)
COLS = LAYERS * (2 * DT + FT)
CONSTS = 13

GAIN = dict(
    trow=UNITS, ttr=UNITS, rcol=UNITS, rrow=2 * UNITS, exp=2 * UNITS, max=2 * UNITS, prob=2 * UNITS,
    av0=SLOTS * T, av0e=SLOTS * T, hT=SLOTS * DT, hTe=SLOTS * DT, ff1=SLOTS * FT, gelu=SLOTS * FT,
    ff2=SLOTS * PARTS, ff2e=SLOTS * PARTS, hn=SLOTS, hres=SLOTS, x=SLOTS, st=SLOTS,
    av1=2 * HEADS, oT=2 * HEADS, back=2 * HEADS, av1e=2 * HEADS, x1T=2 * DT, x1Te=2 * DT, proj=2 * T, xpe=2 * T,
    tneg=2, tall=2, mprep=2, empty=2, m1=2, mT=2 * T, mTe=2 * T, x1=2, out=2, ve=2 * SLOTS + 4, rstd=2 * SLOTS + 4, shift=SLOTS + 2, hmul=SLOTS,
    xin0=16, xin1=16, x0r=32, adj=32, l1ld=64, scrn=32, scrt=32, outst=32, dch=DVE_STEPS,
)

START = dict(av1e=1, outst=16)


class Counts:

    def __init__(self):
        self.n, self.turn, self.value = {name: START.get(name, 0) for name in GAIN}, None, 0

    def skip(self, name, k=1):
        self.n[name] += k

    def __call__(self, name, k=1):
        self.n[name] += k
        return self.n[name] if self.turn is None else self.turn * GAIN[name] + self.n[name]

    def due(self, name, k=1, count=True):
        self.value = self(name, k)
        n = self.n[name]
        if not count:
            self.n[name] -= k
        assert n > 0 or self.turn is None, name
        return n > 0


def pairs(eng, c, body):
    body(0)
    before = dict(c.n)
    with eng.Fori(0, PAIRS - 2) as turn:
        c.turn = turn
        body(turn + 1)
        c.turn = None
    for name, n in c.n.items():
        if n != before[name]:
            assert n - before[name] == GAIN[name], (name, n - before[name], GAIN[name])
            c.n[name] = n + (PAIRS - 3) * GAIN[name]
    body(PAIRS - 1)


def slot_of(k):
    nxt = (k + 1) % SLOTS
    return (k % 2, k // 2), (nxt % 2, nxt // 2)


def late_of(k, l1):
    return heads_of(k - 1, l1)[1:] if k % LAYERS else []


def heads_of(k, l1):
    if not l1:
        return []
    first = sum(HEADS_IN_SLOT[:k])
    return [((first + i) // HEADS, (first + i) % HEADS) for i in range(HEADS_IN_SLOT[k])]


def build(nc, x, adj, attn_w, attn_b, w1, b1, w2, b2, g1, beta1, g2, beta2, w_proj, w_att, b_att, out,
          scr_n, scr_t):
    ctx = ExitStack()
    with ctx:
        def sb(name, shape, dt=F32):
            return ctx.enter_context(nc.sbuf_tensor(name, shape, dt))

        def pb(name, shape, dt=F32):
            return ctx.enter_context(nc.psum_tensor(name, shape, dt))

        w1_sb = sb("w1_sb", [P, LAYERS, DT, FF])
        w2_sb = sb("w2_sb", [P, LAYERS, FT, D])
        wp_sb = sb("wp_sb", [P, DT, D + 2 * HEADS])
        cols = sb("cols", [P, COLS])
        g1_col = cols[:, 0:LAYERS * DT].rearrange("p (l t) -> p l t", l=LAYERS)
        be1_col = cols[:, LAYERS * DT:2 * LAYERS * DT].rearrange("p (l t) -> p l t", l=LAYERS)
        b1_col = cols[:, 2 * LAYERS * DT:].rearrange("p (l t) -> p l t", l=LAYERS)
        g1_row = sb("g1_row", [P, LAYERS, D])
        be1_row = sb("be1_row", [P, LAYERS, D])
        g2_row = sb("g2_row", [P, LAYERS, D])
        be2_row = sb("be2_row", [P, LAYERS, D])
        aw_row = sb("aw_row", [P, LAYERS, 2, D])
        ab_row = sb("ab_row", [P, LAYERS])
        ba_row = sb("ba_row", [P, HEADS])
        ident = sb("ident", [P, P])
        ident_b = sb("ident_b", [P, P], BF16)
        mhalf = sb("mhalf", [P, T])
        xin = [sb(f"xin{s}", [P, T, D + 1]) for s in range(2)]
        xs = [sb(f"xs{s}", [P, T, D + 1]) for s in range(2)]
        mask_n = [sb(f"mask_n{s}", [P, T, N], BF16) for s in range(2)]
        mask_t = [sb(f"mask_t{s}", [P, T, N], BF16) for s in range(2)]
        hT = sb("hT", [P, DT, N])
        G = sb("G", [P, FT, N])
        y_att = sb("y_att", [P, T, D])
        col_rows = y_att[0:COLS, 1, 0:P]
        y_ffn = sb("y_ffn", [P, T, D])
        x0r = sb("x0r", [P, T, D])
        adj_sb = sb("adj_sb", [P, T, N], I32)
        m0 = sb("m0", [P, T, N], BF16)
        m1 = sb("m1", [P, T, N], BF16)
        dge = sb("dge", [P, T, P], BF16)
        diag = sb("diag", [P, T, P], BF16)
        t1_tmp = sb("t1_tmp", [P, T, N], BF16)
        l1n = sb("l1n", [P, T, N], BF16)
        l1t = sb("l1t", [P, T, N], BF16)
        l1x = [sb(f"l1x{s}", [P, T, D]) for s in range(2)]
        oT = sb("oT", [HD + 1, N])
        xp = sb("xp", [P, T, HEADS, HD + 1])
        o1 = sb("o1", [P, T, D])
        outb = sb("outb", [P, T, D])
        prob0 = sb("prob0", [P, T, N])
        prob1 = [sb(f"prob1_{k}", [P, T, N]) for k in range(2)]
        e2 = sb("e2", [P, 2, T // 2, N])
        junk = sb("junk", [P, T, N], BF16)
        junk2 = junk[:].rearrange("p t (a d) -> p t a d", a=2)
        raw0 = sb("raw0", [P, 2, T])
        col0 = sb("col0", [P, 2, T])
        raw1 = sb("raw1", [P, T, 2 * HEADS])
        s1 = sb("s1", [P, T, HEADS])
        t12 = sb("t12", [P, T, HEADS])
        tneg = sb("tneg", [P, HEADS])
        tall = sb("tall", [P, HEADS])
        tmin = sb("tmin", [P, HEADS])
        mx = sb("mx", [P, T])
        z = sb("z", [P, T])
        mrow = sb("mrow", [P, T])
        rcol = [sb(f"rcol{k}", [P, 2, T]) for k in range(2)]
        rec0 = sb("rec0", [P, T])
        rec = sb("rec", [P, T])
        rmax = sb("rmax", [P, T])
        stats = sb("stats", [P, T, 6])
        mv = sb("mv", [P, T, 2])
        veps, rstd = ([sb(f"{name}{i}", [P, T]) for i in range(4)] for name in ("veps", "rstd"))
        nmean, shift = ([sb(f"{name}{i}", [P, T]) for i in range(2)] for name in ("nmean", "shift"))

        ffn = [pb(f"ffn{i}", [P, N]) for i in range(BANKS)]
        trow = pb("trow", [P, N])
        rrow = [pb(f"rrow{i}", [P, N]) for i in range(2)]
        av0 = [pb(f"av0_{i}", [P, N]) for i in range(BANKS)]
        av1 = pb("av1", [P, N])
        mT_ps = [b[:, :].bitcast(BF16).rearrange("p (m t i) -> p m t i", m=2, t=T) for b in av0]
        av1_h = av1[:, 0:T * (HD + 1)].rearrange("p (t k) -> p t k", t=T)
        x1T = prob1[0][:, 0:DT, :]

        def sem(name):
            return ctx.enter_context(nc.semaphore(name))

        s_const, s_wts, s_setup, s_init, s_idn = sem("const"), sem("wts"), sem("setup"), sem("init"), sem("idn")
        s_colT, s_cols = sem("colT"), sem("cols")
        s_xin = [sem("xin0"), sem("xin1")]
        s_x0r, s_adj, s_l1ld = sem("x0r"), sem("adj"), sem("l1ld")
        s_scrn, s_scrt, s_outst = sem("scrn"), sem("scrt"), sem("outst")
        s_empty, s_m1, s_mprep, s_mT, s_mTe = sem("empty"), sem("m1"), sem("mprep"), sem("mT"), sem("mTe")
        s_st, s_trow, s_ttr, s_rcol, s_rrow = sem("st"), sem("trow"), sem("ttr"), sem("rcol"), sem("rrow")
        s_exp, s_max, s_prob = sem("exp"), sem("max"), sem("prob")
        s_av0, s_av0e = sem("av0"), sem("av0e")
        s_av1, s_oT, s_back, s_av1e = sem("av1"), sem("oT"), sem("back"), sem("av1e")
        s_ve, s_rstd, s_shift = sem("ve"), sem("rstd"), sem("shift")
        s_hn, s_hT, s_hTe, s_ff1, s_gelu = sem("hn"), sem("hT"), sem("hTe"), sem("ff1"), sem("gelu")
        s_ff2, s_ff2e, s_hmul, s_hres, s_x = sem("ff2"), sem("ff2e"), sem("hmul"), sem("hres"), sem("x")
        s_x1T, s_x1Te, s_proj, s_xpe = sem("x1T"), sem("x1Te"), sem("proj"), sem("xpe")
        s_tneg, s_tall = sem("tneg"), sem("tall")
        s_x1, s_out = sem("x1"), sem("out")
        s_dch = sem("dch")
        s_passed = sem("passed")
        block = ctx.enter_context(nc.Block())

        def nodes(dram, p, s):
            return dram.rearrange("(g s) (t p) d -> g s p t d", s=2, p=P)[p, s]

        def flat(dram, p, s):
            return dram.rearrange("(g s) p n -> g s p n", s=2)[p, s]

        def is_turn(p, n):
            return isinstance(p, int) and p == n

        def state(s, l):
            return xin[s] if l == 0 else xs[s]

        def probs(kind, head):
            return prob0 if kind == 0 else prob1[head % 2]

        def rows(table, l):
            return table[:, l, :].unsqueeze(1).broadcast_to([P, T, D])

        @block.sync
        def _(sp):
            c = Counts()

            def load_x(p, s):
                sp.dma_start(xin[s][:, :, 0:D], nodes(x, p, s)).then_inc(s_xin[s], 16)

            def load_adj(p, s):
                sp.dma_start(adj_sb[:], nodes(adj, p, s)).then_inc(s_adj, 16)

            def bcast(dst, src):
                sp.dma_start(dst, src.partition_broadcast(P)).then_inc(s_const, 16)

            def rows_in(src, at, n):
                column(col_rows[at:at + n, :], src.rearrange("l (t p) -> (l t) p", p=P))

            def column(dst, src):
                sp.dma_start(dst, src).then_inc(s_const, 16)

            def masks(p, s, then_adj=None):
                sp.wait_ge(s_mprep, c("mprep"))
                sp.sem_inc(s_passed, 1)
                sp.dma_start(flat(scr_n, p, s), mask_n[s][:].rearrange("p t n -> p (t n)")).then_inc(s_scrn, 16)
                if then_adj is not None:
                    load_adj(*then_adj)
                sp.wait_ge(s_mTe, c("mTe", T))
                sp.sem_inc(s_passed, 1)
                sp.dma_start(flat(scr_t, p, s), t1_tmp[:].rearrange("p t n -> p (t n)")).then_inc(s_scrt, 16)

            def load_x0(p, s):
                sp.wait_ge(s_x1, c("x1"))
                sp.sem_inc(s_passed, 1)
                sp.dma_start(x0r[:], nodes(x, p, s)).then_inc(s_x0r, 16)

            def load_l1(p, s, sent=True):
                if s == 0 and sent:
                    sp.wait_ge(s_scrn, c("scrn", 32))
                    sp.sem_inc(s_passed, 1)
                    sp.wait_ge(s_scrt, c("scrt", 32))
                    sp.sem_inc(s_passed, 1)
                sp.wait_ge(s_av1e, c("av1e", HEADS))
                sp.sem_inc(s_passed, 1)
                sp.dma_start(l1n[:].rearrange("p t n -> p (t n)"), flat(scr_n, p, s)).then_inc(s_l1ld, 16)
                sp.dma_start(l1t[:].rearrange("p t n -> p (t n)"), flat(scr_t, p, s)).then_inc(s_l1ld, 16)

            def store_out(p, s):
                sp.wait_ge(s_out, c("out"))
                sp.sem_inc(s_passed, 1)
                sp.dma_start(nodes(out, p, s), outb[:]).then_inc(s_outst, 16)

            sp.sem_inc(s_outst, START["outst"])
            load_adj(0, 0)
            load_x(0, 0)
            bcast(aw_row[:].rearrange("p l a d -> p (l a d)"), attn_w.rearrange("l d -> (l d)"))
            bcast(ab_row[:], attn_b)
            bcast(g1_row[:].rearrange("p l d -> p (l d)"), g1.rearrange("l d -> (l d)"))
            bcast(be1_row[:].rearrange("p l d -> p (l d)"), beta1.rearrange("l d -> (l d)"))
            bcast(g2_row[:].rearrange("p l d -> p (l d)"), g2.rearrange("l d -> (l d)"))
            bcast(be2_row[:].rearrange("p l d -> p (l d)"), beta2.rearrange("l d -> (l d)"))
            bcast(y_ffn[:, 0:LAYERS, :].rearrange("p l d -> p (l d)"), b2.rearrange("l d -> (l d)"))
            bcast(o1[:, 0:2, :].rearrange("p l d -> p (l d)"), w_att.rearrange("l d -> (l d)"))
            bcast(ba_row[:], b_att)
            rows_in(g1, 0, LAYERS * DT)
            rows_in(beta1, LAYERS * DT, LAYERS * DT)
            rows_in(b1, 2 * LAYERS * DT, LAYERS * FT)
            column(wp_sb[:, :, 0:D], w_proj.rearrange("(t p) o -> p t o", p=P))
            for l in range(LAYERS):
                sp.dma_start(w1_sb[:, l], w1[l].rearrange("(t p) f -> p t f", p=P)).then_inc(s_wts, 16)
                sp.dma_start(w2_sb[:, l], w2[l].rearrange("(t p) f -> p t f", p=P)).then_inc(s_wts, 16)
            load_x(0, 1)
            masks(0, 0, then_adj=(0, 1))
            masks(0, 1)
            sp.wait_ge(s_av0e, c("av0e", T))
            sp.sem_inc(s_passed, 1)
            c.skip("scrn", 32)
            c.skip("scrt", 32)
            c.skip("av1e", -HEADS)

            def body(p):
                first, last = is_turn(p, 0), is_turn(p, PAIRS - 1)
                if not last:
                    load_adj(p + 1, 0)
                    load_x(p + 1, 0)
                if first:
                    sp.dma_start(x0r[:], nodes(x, p, 0)).then_inc(s_x0r, 16)
                else:
                    load_l1(p - 1, 0)
                    load_x0(p, 0)
                sp.wait_ge(s_av0e, c("av0e", T))
                sp.sem_inc(s_passed, 1)
                if not last:
                    load_x(p + 1, 1)
                c.skip("av0e", (SLOTS - 1) * T)
                if not first:
                    load_l1(p - 1, 1)
                    store_out(p - 1, 0)
                if not last:
                    masks(p + 1, 0, then_adj=(p + 1, 1))
                load_x0(p, 1)
                if not first:
                    store_out(p - 1, 1)
                if not last:
                    masks(p + 1, 1)

            pairs(sp, c, body)
            load_l1(PAIRS - 1, 0, sent=False)
            load_l1(PAIRS - 1, 1)
            store_out(PAIRS - 1, 0)
            store_out(PAIRS - 1, 1)
            sp.wait_ge(s_outst, START["outst"] + 16 * GRAPHS)
            sp.wait_ge(s_scrn, 16 * GRAPHS)
            sp.wait_ge(s_scrt, 16 * GRAPHS)

        @block.gpsimd
        def _(pool):
            c = Counts()
            nc.gpsimd.memset(ident[:], 0.0).then_inc(s_idn, 1)
            nc.gpsimd.memset(ident_b[:], 0.0).then_inc(s_idn, 1)
            nc.gpsimd.memset(mhalf[:], -0.5).then_inc(s_idn, 1)
            pool.wait_ge(s_idn, 3)
            for m in (ident, ident_b):
                nc.gpsimd.affine_select(out=m[:], in_=m[:], compare_op=ALU.not_equal, fill=1.0, base=0,
                                        pattern=[[-1, P]], channel_multiplier=1).then_inc(s_idn, 1)
            pool.wait_ge(s_const, 16 * CONSTS)
            pool.wait_ge(s_setup, 1)

            def inverse_deviation(which):
                pool.wait_ge(s_ve, c("ve"))
                nc.gpsimd.tensor_tensor(rstd[which][:], veps[which][:], mhalf[:], ALU.pow).then_inc(s_rstd, 1)
                if which not in (ATTENDED, RESIDUAL):
                    c.skip("rstd")
                else:
                    pool.wait_ge(s_rstd, c("rstd"))
                    nc.gpsimd.tensor_tensor(shift[which][:], nmean[which][:], rstd[which][:], ALU.mult).then_inc(s_shift, 1)

            def residual(s, l):
                h = xs[s][:, :, 0:D]
                pool.wait_ge(s_hT, c("hT", DT))
                nc.gpsimd.tensor_tensor(h, h, rows(g1_row, l), ALU.mult).then_inc(s_hmul, 1)
                pool.wait_ge(s_hmul, c("hmul"))
                nc.gpsimd.tensor_tensor(h, h, rows(be1_row, l), ALU.add).then_inc(s_hres, 1)

            def least_targets():
                pool.wait_ge(s_tneg, c("tneg"))
                pool.sem_inc(s_passed, 1)
                nc.gpsimd.partition_all_reduce(tall[:], tneg[:], P, RMAX).then_inc(s_tall, 1)

            inverse_deviation(ATTENDED)

            def body(p):
                first, last = is_turn(p, 0), is_turn(p, PAIRS - 1)
                for k in range(SLOTS):
                    (s, l), (s2, l2) = slot_of(k)
                    if not (first and k == 0):
                        inverse_deviation(FED)
                    residual(s, l)
                    if k in (0, 3) and not first:
                        least_targets()
                    if k == SLOTS - 1 or (k == 0 and not first):
                        inverse_deviation(RESIDUAL)
                    if not (last and k == SLOTS - 1):
                        inverse_deviation(ATTENDED)
                    if k in (2, 5) and not first:
                        inverse_deviation(LAST)

            pairs(pool, c, body)
            inverse_deviation(FED)
            inverse_deviation(RESIDUAL)
            for s in range(2):
                least_targets()
                inverse_deviation(LAST)

        @block.scalar
        def _(act):
            c = Counts()
            c.skip("max", -2)
            c.skip("av0", -T)
            c.skip("scrt", -16)
            act.wait_ge(s_colT, 1)
            nc.scalar.copy(cols[:], ffn[0][:, 0:COLS]).then_inc(s_cols, 1)
            act.wait_ge(s_cols, 1)

            def exps(kind, head=None):
                if kind == 0:
                    if c.due("av0", T):
                        act.wait_ge(s_av0, c.value)
                    t, t2 = raw0[:, 1, :], col0[:, 1, :]
                else:
                    t, t2 = raw1[:, :, HEADS + head], t12[:, :, head]
                for half in range(2):
                    tiles = range(half * T // 2, (half + 1) * T // 2)
                    if half == 0:
                        act.wait_ge(s_rrow, c("rrow"))
                    for j in tiles:
                        nc.scalar.activation(probs(kind, head)[:, j, :], rrow[0][:], ACT.Exp, bias=t[:, j:j + 1])
                    if half == 0:
                        act.wait_ge(s_rrow, c("rrow"))
                    if c.due("max"):
                        act.wait_ge(s_max, c.value)
                    for j in tiles:
                        last = nc.scalar.activation(e2[:, half, j % 2, :], rrow[1][:], ACT.Exp, bias=t2[:, j:j + 1])
                    last.then_inc(s_exp, 1)

            def transposed(dt, l):
                act.wait_ge(s_hT, c("hT"))
                nc.scalar.activation(hT[:, dt, :], av0[dt][:], ACT.Identity, bias=be1_col[:, l, dt:dt + 1],
                                     scale=g1_col[:, l, dt:dt + 1]).then_inc(s_hTe, 1)

            def gelu(l, f):
                act.wait_ge(s_ff1, c("ff1"))
                nc.scalar.activation(G[:, f, :], ffn[f % BANKS][:], ACT.Gelu,
                                     bias=b1_col[:, l, f:f + 1]).then_inc(s_gelu, 1)

            def head_rows():
                act.wait_ge(s_av1, c("av1"))
                nc.scalar.copy(oT[:], av1[0:HD + 1, :]).then_inc(s_oT, 1)

            def second_mask():
                act.wait_ge(s_empty, c("empty"))
                for t in range(T):
                    last = nc.scalar.activation(m1[:, t, :], m0[:, t, :], ACT.Identity, bias=rmax[:, t:t + 1])
                last.then_inc(s_m1, 1)

            def masks(s):
                if c.due("scrt", 16):
                    act.wait_ge(s_scrt, c.value)
                for i in range(T):
                    act.wait_ge(s_mT, c("mT"))
                    nc.scalar.copy(mask_t[s][:, :, i * P:(i + 1) * P], mT_ps[i % BANKS][:, 0])
                    nc.scalar.copy(t1_tmp[:, :, i * P:(i + 1) * P], mT_ps[i % BANKS][:, 1]).then_inc(s_mTe, 1)

            def normalise(which, src, dst, done):
                act.wait_ge(s_shift, c("shift"))
                for t in range(T):
                    last = nc.scalar.activation(dst[:, t, 0:D], src[:, t, :], ACT.Identity, bias=shift[which][:, t:t + 1],
                                                scale=rstd[which][:, t:t + 1])
                last.then_inc(done, 1)

            def state_out(dt):
                act.wait_ge(s_x1T, c("x1T"))
                nc.scalar.copy(x1T[:, dt, :], av1[:]).then_inc(s_x1Te, 1)

            def values_out(t):
                act.wait_ge(s_proj, c("proj"))
                nc.scalar.copy(xp[:, t, :, 0:HD], av1[:, 0:D].rearrange("p (h k) -> p h k", h=HEADS))
                nc.scalar.copy(raw1[:, t, :], av1[:, D:D + 2 * HEADS]).then_inc(s_xpe, 1)

            def graph_begins():
                for dt in range(DT):
                    state_out(dt)
                for t in range(T):
                    values_out(t)

            second_mask()
            masks(0)
            exps(0)
            normalise(ATTENDED, y_att, xs[0], s_hn)
            for dt in range(DT):
                transposed(dt, 0)

            def body(p):
                first, last = is_turn(p, 0), is_turn(p, PAIRS - 1)
                for k in range(SLOTS):
                    (s, l), (s2, l2) = slot_of(k)
                    for f in range(FT):
                        if not first and k in (0, 3):
                            if f < DT:
                                state_out(f)
                            elif f < DT + T:
                                values_out(f - DT)
                        if first and k == 0 and f == BANKS:
                            second_mask()
                            masks(1)
                        gelu(l, f)
                    att = not (last and k == SLOTS - 1)
                    heads = heads_of(k, not first)
                    if att:
                        exps(0)
                    late = late_of(k, not first)
                    if late:
                        head_rows()
                    if heads:
                        exps(1, heads[0][1])
                    if k == SLOTS - 1 or (k == 0 and not first):
                        normalise(RESIDUAL, y_ffn, l1x[1 - s], s_x1)
                    if len(late) > 1:
                        head_rows()
                    if heads:
                        exps(1, heads[1][1])
                    if not last and k in (4, 5):
                        second_mask()
                    if heads:
                        head_rows()
                    if not last and k in (4, 5):
                        masks(k - 4)
                    if att:
                        normalise(ATTENDED, y_att, xs[s2], s_hn)
                    if heads and k % LAYERS == LAYERS - 1:
                        head_rows()
                    if att:
                        for dt in range(DT):
                            transposed(dt, l2)
                    if len(heads) > 2:
                        exps(1, heads[2][1])

            pairs(act, c, body)
            for s in range(2):
                graph_begins()
                if s == 0:
                    normalise(RESIDUAL, y_ffn, l1x[1], s_x1)
                exps(1, 0)
                for head in range(HEADS):
                    if head + 1 < HEADS:
                        exps(1, head + 1)
                    head_rows()

        @block.vector
        def _(dve):
            c = Counts()
            c.skip("scrn", -32)
            c.skip("outst", -16)
            v = nc.vector

            def statistics(which, src):
                for t in range(T):
                    last = v.bn_stats(stats[:, t, :], src[:, t, 0:D])
                last.then_inc(s_dch, 1)
                dve.wait_ge(s_dch, c("dch"))
                dve.sem_inc(s_passed, 1)
                for t in range(T):
                    last = v.bn_aggr(mv[:, t, :], stats[:, t, :])
                last.then_inc(s_dch, 1)
                dve.wait_ge(s_dch, c("dch"))
                if which in (ATTENDED, RESIDUAL):
                    v.tensor_scalar(nmean[which][:], mv[:, :, 0], -1.0, None, ALU.mult)
                v.tensor_scalar_add(veps[which][:], mv[:, :, 1], EPS).then_inc(s_ve, 1)

            def make_masks(s):
                dve.wait_ge(s_adj, c("adj", 16))
                if c.due("scrn", 16):
                    dve.wait_ge(s_scrn, c.value)
                v.tensor_scalar(m0[:], adj_sb[:], 0.0, None, ALU.is_gt).then_inc(s_dch, 1)
                dve.wait_ge(s_dch, c("dch"))
                v.tensor_scalar(mask_n[s][:], m0[:], -1.0, BIG, ALU.add, ALU.mult)
                v.tensor_reduce(rmax[:], m0[:], AX.X, ALU.max).then_inc(s_dch, 1)
                dve.wait_ge(s_dch, c("dch"))
                v.tensor_scalar(rmax[:], rmax[:], 0.0, None, ALU.is_le).then_inc(s_empty, 1)

            def make_diagonal():
                for t in range(T):
                    last = v.scalar_tensor_tensor(dge[:, t, :], adj_sb[:, t, t * P:(t + 1) * P], 0.0, ident_b[:],
                                                  ALU.is_ge, ALU.mult)
                last.then_inc(s_dch, 1)
                dve.wait_ge(s_dch, c("dch"))
                for t in range(T):
                    last = v.tensor_tensor(diag[:, t, :], m0[:, t, t * P:(t + 1) * P], dge[:, t, :], ALU.max)
                last.then_inc(s_mprep, 1)

            def scores(s, l):
                if l == 0:
                    dve.wait_ge(s_xin[s], c(f"xin{s}", 16))
                for a in range(2):
                    for t in range(T):
                        last = v.tensor_tensor_reduce(out=junk2[:, t, a, :], in0=state(s, l)[:, t, 0:D], in1=aw_row[:, l, a, :],
                                                      scale=1.0, scalar=0.0, op0=ALU.mult, op1=ALU.add,
                                                      accum_out=raw0[:, a, t:t + 1])
                last.then_inc(s_st, 1)
                dve.wait_ge(s_st, c("st"))
                v.tensor_scalar(col0[:, 0, :], raw0[:, 0, :], ab_row[:, l:l + 1], None, ALU.add)
                v.tensor_scalar(col0[:, 1, :], raw0[:, 1, :], SLOPE, None, ALU.mult).then_inc(s_dch, 1)
                dve.wait_ge(s_dch, c("dch"))

            def row_maxima(kind, s=None, head=None):
                mask = mask_n[s] if kind == 0 else l1n
                src = col0[:, 0, :] if kind == 0 else s1[:, :, head]
                least = -3.0e38 if kind == 0 else tmin[:, head:head + 1]
                dve.wait_ge(s_trow, c("trow"))
                dve.sem_inc(s_passed, 1)
                for t in range(T):
                    last = v.tensor_tensor_reduce(out=junk[:, t, :], in0=trow[:], in1=mask[:, t, :], scale=1.0,
                                                  scalar=least, op0=ALU.add, op1=ALU.max, accum_out=mx[:, t:t + 1])
                last.then_inc(s_ttr, 1)
                dve.wait_ge(s_ttr, c("ttr"))
                if kind == 0:
                    v.tensor_tensor(mx[:], mx[:], raw0[:, 1, :], ALU.max).then_inc(s_dch, 1)
                    dve.wait_ge(s_dch, c("dch"))
                v.tensor_tensor(z[:], mx[:], src, ALU.add).then_inc(s_dch, 1)
                dve.wait_ge(s_dch, c("dch"))
                v.scalar_tensor_tensor(mrow[:], z[:], SLOPE, z[:], ALU.mult, ALU.max).then_inc(s_dch, 1)
                dve.wait_ge(s_dch, c("dch"))
                v.tensor_tensor(rcol[kind][:, 0, :], src, mrow[:], ALU.subtract)
                v.scalar_tensor_tensor(rcol[kind][:, 1, :], src, SLOPE, mrow[:], ALU.mult,
                                       ALU.subtract).then_inc(s_rcol, 1)

            def combine(kind, s=None, head=None):
                p = probs(kind, head)
                mask = mask_t[s] if kind == 0 else l1t
                for half in range(2):
                    j = slice(half * T // 2, (half + 1) * T // 2)
                    dve.wait_ge(s_exp, c("exp"))
                    v.tensor_tensor(p[:, j, :], p[:, j, :], e2[:, half], ALU.max).then_inc(s_max, 1)
                    dve.wait_ge(s_max, c("max"))
                    v.tensor_tensor(p[:, j, :], p[:, j, :], mask[:, j, :], ALU.min).then_inc(s_prob, 1)

            def attended(s, l, t):
                bank = av0[t % BANKS]
                dve.wait_ge(s_av0, c("av0"))
                v.reciprocal(rec0[:, t:t + 1], bank[:, D:D + 1]).then_inc(s_dch, 1)
                dve.wait_ge(s_dch, c("dch"))
                v.scalar_tensor_tensor(y_att[:, t, :], bank[:, 0:D], rec0[:, t:t + 1], state(s, l)[:, t, 0:D], ALU.mult,
                                       ALU.add).then_inc(s_av0e, 1)

            def norm_attended():
                dve.wait_ge(s_av0e, c("av0e", T))
                statistics(ATTENDED, y_att)
                c.skip("rstd")

            def fed_forward(s, part):
                if part == 0:
                    dve.wait_ge(s_hres, c("hres"))
                dve.wait_ge(s_ff2, c("ff2"))
                t = slice(part * T // PARTS, (part + 1) * T // PARTS)
                v.tensor_tensor(y_ffn[:, t, :], ffn[part][:].rearrange("p (t d) -> p t d", d=D), xs[s][:, t, 0:D],
                                ALU.add).then_inc(s_ff2e, 1)

            def layer_ends(s, l):
                dve.wait_ge(s_ff2e, c("ff2e", PARTS))
                statistics(FED, y_ffn)
                for t in range(T):
                    last = v.scalar_tensor_tensor(y_ffn[:, t, :], y_ffn[:, t, :], mv[:, t, 0:1], g2_row[:, l, :],
                                                  ALU.subtract, ALU.mult)
                last.then_inc(s_dch, 1)
                dve.wait_ge(s_dch, c("dch"))
                dve.wait_ge(s_rstd, c("rstd"))
                for t in range(T):
                    last = v.scalar_tensor_tensor(xs[s][:, t, 0:D], y_ffn[:, t, :], rstd[FED][:, t:t + 1],
                                                  be2_row[:, l, :], ALU.mult, ALU.add)
                last.then_inc(s_x, 1)
                dve.wait_ge(s_x, c("x"))

            def first_network_ends(s):
                dve.wait_ge(s_x0r, c("x0r", 16))
                v.tensor_tensor(y_ffn[:], xs[s][:, :, 0:D], x0r[:], ALU.add).then_inc(s_dch, 1)
                dve.wait_ge(s_dch, c("dch"))
                statistics(RESIDUAL, y_ffn)
                c.skip("rstd")

            def graph_begins():
                dve.wait_ge(s_l1ld, c("l1ld", 32))
                dve.wait_ge(s_xpe, c("xpe", T))
                v.tensor_tensor(s1[:], raw1[:, :, 0:HEADS], ba_row[:].unsqueeze(1).broadcast_to([P, T, HEADS]),
                                ALU.add).then_inc(s_dch, 1)
                dve.wait_ge(s_dch, c("dch"))
                v.tensor_scalar(t12[:], raw1[:, :, HEADS:], SLOPE, None, ALU.mult)
                v.tensor_reduce(tmin[:], raw1[:, :, HEADS:].rearrange("p t h -> p h t"), AX.X, ALU.min).then_inc(s_dch, 1)
                dve.wait_ge(s_dch, c("dch"))
                v.tensor_scalar(tneg[:], tmin[:], -1.0, None, ALU.mult).then_inc(s_tneg, 1)
                dve.wait_ge(s_tall, c("tall"))
                v.tensor_scalar(tmin[:], tall[:], -1.0, None, ALU.mult).then_inc(s_dch, 1)
                dve.wait_ge(s_dch, c("dch"))

            def head_out(head):
                dve.wait_ge(s_back, c("back"))
                v.reciprocal(rec[:], av1_h[:, :, HD]).then_inc(s_dch, 1)
                dve.wait_ge(s_dch, c("dch"))
                v.tensor_tensor(o1[:, :, head * HD:(head + 1) * HD], av1_h[:, :, 0:HD],
                                rec[:].unsqueeze(2).broadcast_to([P, T, HD]), ALU.mult).then_inc(s_av1e, 1)

            def graph_ends(s):
                dve.wait_ge(s_av1e, c("av1e", HEADS))
                v.scalar_tensor_tensor(o1[:], o1[:], 0.0, l1x[s][:], ALU.max, ALU.add).then_inc(s_dch, 1)
                dve.wait_ge(s_dch, c("dch"))
                if c.due("outst", 16):
                    dve.wait_ge(s_outst, c.value)
                statistics(LAST, o1)
                dve.wait_ge(s_rstd, c("rstd"))
                for t in range(T):
                    last = v.tensor_scalar(outb[:, t, :], o1[:, t, :], mv[:, t, 0:1], rstd[LAST][:, t:t + 1],
                                           ALU.subtract, ALU.mult)
                last.then_inc(s_out, 1)

            dve.sem_inc(s_av1e, START["av1e"])
            for b in xin + xs:
                v.memset(b[:, :, D:D + 1], 1.0)
            v.memset(xp[:, :, :, HD:HD + 1], 1.0).then_inc(s_init, 1)
            dve.wait_ge(s_idn, 5)
            make_masks(0)
            make_diagonal()
            dve.wait_ge(s_const, 16 * CONSTS)
            watt = o1[:, 0:2, :].rearrange("p a d -> p (a d)").rearrange("p (h a k) -> p h a k", h=HEADS, a=2)
            prod = y_att[:, 0, :].rearrange("p (h k) -> p h k", h=HEADS)
            for dt in range(DT):
                for a in range(2):
                    v.tensor_tensor(prod, wp_sb[:, dt, 0:D].rearrange("p (h k) -> p h k", h=HEADS),
                                    watt[:, :, a, :], ALU.mult).then_inc(s_dch, 1)
                    dve.wait_ge(s_dch, c("dch"))
                    v.tensor_reduce(wp_sb[:, dt, D + a * HEADS:D + (a + 1) * HEADS], prod, AX.X, ALU.add).then_inc(s_dch, 1)
                    dve.wait_ge(s_dch, c("dch"))
            v.tensor_tensor(be1_row[:], be1_row[:], y_ffn[:, 0:LAYERS, :], ALU.add).then_inc(s_setup, 1)
            scores(0, 0)
            row_maxima(0, 0)
            dve.wait_ge(s_mTe, c("mTe", T))
            combine(0, 0)
            for t in range(T):
                attended(0, 0, t)
            norm_attended()
            make_masks(1)
            make_diagonal()

            def body(p):
                first, last = is_turn(p, 0), is_turn(p, PAIRS - 1)
                for k in range(SLOTS):
                    (s, l), (s2, l2) = slot_of(k)
                    heads = heads_of(k, not first)
                    att = not (last and k == SLOTS - 1)
                    if not (first and k == 0):
                        layer_ends(1 - s, (k - 1) % SLOTS // 2)
                    late = late_of(k, not first)
                    if att:
                        scores(s2, l2)
                        row_maxima(0, s2)
                    ends = k == SLOTS - 1 or (k == 0 and not first)
                    if heads and k in (0, 3):
                        graph_begins()
                    if len(late) > 1:
                        combine(1, head=late[1][1])
                    if heads:
                        row_maxima(1, head=heads[0][1])
                    if ends:
                        first_network_ends(1 - s)
                    if late:
                        head_out(late[0][1])
                    if att:
                        if l2 == 0:
                            dve.wait_ge(s_mTe, c("mTe", T))
                        combine(0, s2)
                    if heads:
                        row_maxima(1, head=heads[1][1])
                    new_masks = not last and k in (4, 5)
                    if new_masks:
                        make_masks(k - 4)
                    if att:
                        attended(s2, l2, 0)
                        attended(s2, l2, 1)
                    if len(late) > 1:
                        head_out(late[1][1])
                    if heads:
                        combine(1, head=heads[0][1])
                    if new_masks:
                        make_diagonal()
                    if len(heads) > 2:
                        row_maxima(1, head=heads[2][1])
                    if att:
                        attended(s2, l2, 2)
                        attended(s2, l2, 3)
                        norm_attended()
                    if ends:
                        dve.wait_ge(s_x1, c("x1"))
                    fed_forward(s, 0)
                    if heads:
                        combine(1, head=heads[1][1])
                        head_out(heads[0][1])
                    if heads and k % LAYERS == LAYERS - 1:
                        head_out(heads[1][1])
                        graph_ends(heads[1][0])
                    fed_forward(s, 1)

            pairs(dve, c, body)
            layer_ends(1, LAYERS - 1)
            first_network_ends(1)
            for s in range(2):
                if s == 1:
                    dve.wait_ge(s_x1, c("x1"))
                graph_begins()
                row_maxima(1, head=0)
                row_maxima(1, head=1)
                for head in range(HEADS):
                    combine(1, head=head)
                    if head > 0:
                        head_out(head - 1)
                    if head + 2 < HEADS:
                        row_maxima(1, head=head + 2)
                head_out(HEADS - 1)
                graph_ends(s)

        @block.tensor
        def _(pe):
            c = Counts()
            c.skip("ff2e", -BANKS)
            c.skip("ttr", -1)
            c.skip("exp", -2)
            c.skip("av0e", -BANKS)
            c.skip("mTe", -BANKS)
            c.skip("av1e", -1)
            te = nc.tensor

            def spread(row, col):
                for t in range(T):
                    last = te.transpose(row[:, t * P:(t + 1) * P], col[:, t:t + 1].broadcast_to([P, P]), ident[:])
                return last

            def target_row(kind, head=None):
                if kind == 0:
                    pe.wait_ge(s_st, c("st"))
                if c.due("ttr"):
                    pe.wait_ge(s_ttr, c.value)
                spread(trow, raw0[:, 1, :] if kind == 0 else raw1[:, :, HEADS + head]).then_inc(s_trow, 1)

            def exp_rows(kind):
                pe.wait_ge(s_rcol, c("rcol"))
                if c.due("exp", 2):
                    pe.wait_ge(s_exp, c.value)
                for a in range(2):
                    spread(rrow[a], rcol[kind][:, a, :]).then_inc(s_rrow, 1)

            def attend(s, l, t):
                if t == 0:
                    pe.wait_ge(s_prob, c("prob", 2))
                    if c.due("mTe", BANKS, count=False):
                        pe.wait_ge(s_mTe, c.value)
                    if l == 0:
                        pe.wait_ge(s_xin[s], c(f"xin{s}", 16))
                if c.due("av0e"):
                    pe.wait_ge(s_av0e, c.value)
                for j in range(T):
                    last = te.matmul(av0[t % BANKS][:, 0:D + 1], prob0[:, j, t * P:(t + 1) * P], state(s, l)[:, j, :],
                                     start=j == 0, stop=j == T - 1)
                last.then_inc(s_av0, 1)

            def attend_head(head):
                if head == 0:
                    pe.wait_ge(s_xpe, c("xpe"))
                pe.wait_ge(s_prob, c("prob", 2))
                pe.wait_ge(s_av1e, c("av1e"))
                for j in range(T):
                    last = te.matmul(av1[0:HD + 1, :], xp[:, j, head, :], prob1[head % 2][:, j, :],
                                     start=j == 0, stop=j == T - 1)
                last.then_inc(s_av1, 1)

            def head_back():
                pe.wait_ge(s_oT, c("oT"))
                pe.sem_inc(s_passed, 1)
                for t in range(T):
                    last = te.transpose(av1_h[:, t, :], oT[:, t * P:(t + 1) * P], ident[0:HD + 1, 0:HD + 1])
                last.then_inc(s_back, 1)

            def transpose_state(s, dt):
                if dt == 0:
                    if c.due("mTe", BANKS, count=False):
                        pe.wait_ge(s_mTe, c.value)
                    pe.wait_ge(s_hn, c("hn"))
                for t in range(T):
                    last = te.transpose(av0[dt][:, t * P:(t + 1) * P], xs[s][:, t, dt * P:(dt + 1) * P], ident[:])
                last.then_inc(s_hT, 1)

            def first_product(l, f):
                if f == 0:
                    pe.wait_ge(s_hTe, c("hTe", DT))
                if f < BANKS:
                    if c.due("ff2e"):
                        pe.wait_ge(s_ff2e, c.value)
                else:
                    pe.wait_ge(s_gelu, c("gelu"))
                for dt in range(DT):
                    last = te.matmul(ffn[f % BANKS][:], w1_sb[:, l, dt, f * P:(f + 1) * P], hT[:, dt, :],
                                     start=dt == 0, stop=dt == DT - 1)
                last.then_inc(s_ff1, 1)

            def second_product(l, t, quarter=None):
                if t == 0 and not quarter:
                    pe.wait_ge(s_gelu, c("gelu", BANKS))
                part, at = t // (T // PARTS), t % (T // PARTS) * D
                for f in range(FT) if quarter is None else range(quarter * FT // 4, (quarter + 1) * FT // 4):
                    last = te.matmul(ffn[part][:, at:at + D], G[:, f, t * P:(t + 1) * P], w2_sb[:, l, f, :],
                                     start=f == 0, stop=f == FT - 1)
                if at + D == T // PARTS * D and f == FT - 1:
                    last.then_inc(s_ff2, 1)

            def masks(other=None):
                pe.wait_ge(s_mprep, c("mprep"))
                pe.wait_ge(s_m1, c("m1"))
                for i in range(T):
                    if i == 0:
                        if c.due("av0e", BANKS, count=False):
                            pe.wait_ge(s_av0e, c.value)
                    if c.due("mTe"):
                        pe.wait_ge(s_mTe, c.value)
                    for m, src in enumerate((m0, m1)):
                        for j in range(T):
                            last = te.transpose(mT_ps[i % BANKS][:, m, j, :],
                                                diag[:, i, :] if m == 0 and i == j else src[:, i, j * P:(j + 1) * P],
                                                ident_b[:])
                    last.then_inc(s_mT, 1)
                    if other is not None:
                        other(i)

            def state_in(s, dt):
                if dt == 0:
                    pe.wait_ge(s_x1, c("x1"))
                    if c.due("av1e", count=False):
                        pe.wait_ge(s_av1e, c.value)
                else:
                    pe.wait_ge(s_x1Te, c("x1Te"))
                for t in range(T):
                    last = te.transpose(av1[:, t * P:(t + 1) * P], l1x[s][:, t, dt * P:(dt + 1) * P], ident[:])
                last.then_inc(s_x1T, 1)

            def project(t):
                if t == 0:
                    pe.wait_ge(s_x1Te, c("x1Te"))
                else:
                    pe.wait_ge(s_xpe, c("xpe"))
                for dt in range(DT):
                    last = te.matmul(av1[:, 0:D + 2 * HEADS], x1T[:, dt, t * P:(t + 1) * P], wp_sb[:, dt, :],
                                     start=dt == 0, stop=dt == DT - 1)
                last.then_inc(s_proj, 1)

            pe.wait_ge(s_idn, 5)
            pe.wait_ge(s_init, 1)
            pe.wait_ge(s_const, 16 * CONSTS)
            te.transpose(ffn[0][:, 0:COLS], col_rows, ident[0:COLS, 0:COLS]).then_inc(s_colT, 1)
            masks()
            target_row(0)
            exp_rows(0)
            for t in range(T):
                attend(0, 0, t)
            for dt in range(DT):
                transpose_state(0, dt)
            pe.wait_ge(s_cols, 1)
            pe.wait_ge(s_setup, 1)
            pe.wait_ge(s_wts, 16 * 2 * LAYERS)

            def body(p):
                first, last = is_turn(p, 0), is_turn(p, PAIRS - 1)
                for k in range(SLOTS):
                    (s, l), (s2, l2) = slot_of(k)
                    heads = heads_of(k, not first)
                    late = late_of(k, not first)
                    att = not (last and k == SLOTS - 1)
                    for f in range(FT):
                        if not first and k in (0, 3):
                            if f < DT:
                                state_in(k // 3, f)
                            elif f < DT + T:
                                project(f - DT)
                        if first and k == 0 and f == BANKS:
                            masks()
                        if f == 5 and att:
                            target_row(0)
                        if f == FT - 1 and heads:
                            if k in (0, 3):
                                if c.due("xpe", count=False):
                                    pe.wait_ge(s_xpe, c.value)
                            target_row(1, heads[0][1])
                        first_product(l, f)
                    if att:
                        exp_rows(0)
                    if late:
                        attend_head(late[0][1])
                    second_product(l, 0)
                    if late:
                        head_back()
                    if k in (0, 3) or first:
                        second_product(l, 1)
                    if heads:
                        exp_rows(1)
                        target_row(1, heads[1][1])
                    if len(late) > 1:
                        attend_head(late[1][1])
                    if att:
                        attend(s2, l2, 0)
                        attend(s2, l2, 1)
                    if len(late) > 1:
                        head_back()
                    if heads:
                        exp_rows(1)
                    if len(heads) > 2:
                        target_row(1, heads[2][1])
                    if not (k in (0, 3) or first):
                        second_product(l, 1)
                    if att:
                        attend(s2, l2, 2)
                        attend(s2, l2, 3)
                    if heads:
                        attend_head(heads[0][1])
                    if not last and k in (4, 5):
                        masks(lambda i: second_product(l, 2, i))
                    else:
                        second_product(l, 2)
                    if heads:
                        head_back()
                    if len(heads) > 2:
                        exp_rows(1)
                    if heads and k % LAYERS == LAYERS - 1:
                        attend_head(heads[1][1])
                    if att:
                        for dt in range(DT):
                            transpose_state(s2, dt)
                    if heads and k % LAYERS == LAYERS - 1:
                        head_back()
                    second_product(l, 3)

            pairs(pe, c, body)
            for s in range(2):
                for dt in range(DT):
                    state_in(s, dt)
                for t in range(T):
                    project(t)
                if c.due("xpe", count=False):
                    pe.wait_ge(s_xpe, c.value)
                target_row(1, 0)
                exp_rows(1)
                target_row(1, 1)
                for head in range(HEADS):
                    if head + 1 < HEADS:
                        exp_rows(1)
                    if head + 2 < HEADS:
                        target_row(1, head + 2)
                    attend_head(head)
                    head_back()


_INS = ["x", "adj", "L0_gnn_attn_w", "L0_gnn_attn_b", "L0_gnn_W1", "L0_gnn_b1", "L0_gnn_W2", "L0_gnn_b2",
        "L0_gnn_g1", "L0_gnn_beta1", "L0_gnn_g2", "L0_gnn_beta2", "L1_gnn_W_proj", "L1_gnn_W_att", "L1_gnn_b_att"]


def kernel(**inputs):
    import numpy as np
    import concourse.bacc as bacc
    from concourse.bass_utils import run_bass_kernel_spmd as run

    nc = bacc.Bacc("TRN2", target_bir_lowering=False, num_devices=1, dynamic_dma_scratch_size=1024)
    arrays, args = {}, []
    for name in _INS:
        a = np.ascontiguousarray(inputs[name])
        arrays[f"in_{name}"] = a
        args.append(nc.dram_tensor(f"in_{name}", a.shape, mybir.dt.from_np(a.dtype), kind="ExternalInput").ap())
    out = nc.dram_tensor("out_0", (GRAPHS, N, D), F32, kind="ExternalOutput").ap()
    scr_n = nc.dram_tensor("scr_n", (GRAPHS, P, T * N), BF16, kind="Internal").ap()
    scr_t = nc.dram_tensor("scr_t", (GRAPHS, P, T * N), BF16, kind="Internal").ap()
    build(nc, *args, out, scr_n, scr_t)
    r = run(nc, [arrays], core_ids=[0])
    return r.results[0]["out_0"]
```
